# Optimizing a Trainium2 kernel written in Bass

```python
import numpy as np
import jax
import jax.numpy as jnp

def _softmax(x, axis=-1):
    return jax.nn.softmax(x, axis=axis)

def _gelu(x):
    return jax.nn.gelu(x, approximate=True)

def _silu(x):
    return jax.nn.silu(x)

def _sigmoid(x):
    return jax.nn.sigmoid(x)

def _layernorm(x, axis=-1, eps=1e-05):
    m = jnp.mean(x, axis=axis, keepdims=True)
    v = jnp.var(x, axis=axis, keepdims=True)
    return (x - m) / jnp.sqrt(v + eps)

def _scatter_add(tgt, idx, src, axis=0):
    return tgt.at[idx].add(src)

def _segment_sum(src, seg, n):
    return jax.ops.segment_sum(src, seg, n)
kernel_name = 'mk_adj_resnorm_d2_adj_r2_af69b3'

def setup_inputs(seed: int=0):
    np.random.seed(seed)
    _w = jnp.asarray

    def _rec_inputs():
        import jax
        import jax.numpy as jnp
        _gk = jax.random.key(seed)
        x = -0.000929 + 1 * jax.random.normal(jax.random.fold_in(_gk, 1), (8, 2048, 64), jnp.float32)
        _a = jax.random.bernoulli(jax.random.fold_in(_gk, 2), 0.000976562, (8, 2048, 2048))
        _a = jnp.logical_or(_a, jnp.eye(2048, dtype=bool))
        _af = _a.astype(jnp.float32)
        _af = _af * jax.random.uniform(jax.random.fold_in(_gk, 3), (8, 2048, 2048), jnp.float32, 0.05, 1)
        adj = _af
        return (x, adj)
    x, adj = _rec_inputs()

    def _L0_gnn_setup():
        import jax, jax.numpy as jnp
        import numpy as np
        B, N, C, R = (4, 2048, 64, 16)
        EPS = 1e-12
        key = jax.random.key(seed)
        k_x, k_w, k_u = jax.random.split(key, 3)
        x = jax.random.normal(k_x, (B, N, C), dtype=jnp.float32)
        W = jax.random.uniform(k_w, (B, N, N), dtype=jnp.float32)
        U = 0.01 * jax.random.normal(k_u, (N, R), dtype=jnp.float32)
        w_scale = jnp.asarray(1.0, dtype=jnp.float32)
        return {'x': x, 'W': W, 'U': U, 'w_scale': w_scale}
    _L0_gnn_all = _L0_gnn_setup()
    _L0_gnn_in = {k: v for k, v in _L0_gnn_all.items() if k in ('U', 'w_scale')}
    del _L0_gnn_all

    def _L1_gnn_setup():
        import jax, jax.numpy as jnp
        import numpy as np
        key = jax.random.key(seed)
        k1, k2 = jax.random.split(key)
        B, N, D = (16, 1024, 64)
        nodes = jax.random.normal(k1, (B, N, D), dtype=jnp.float32)
        edges = jax.random.uniform(k2, (B, N, N), dtype=jnp.float32)
        return {'nodes': nodes, 'edges': edges}
    _L1_gnn_all = _L1_gnn_setup()
    _L1_gnn_in = {k: v for k, v in _L1_gnn_all.items() if k in ()}
    del _L1_gnn_all
    return {'x': x, 'adj': adj, 'L0_gnn_U': _L0_gnn_in['U'], 'L0_gnn_w_scale': _L0_gnn_in['w_scale']}

def reference(x, adj, L0_gnn_U, L0_gnn_w_scale):
    import jax
    import jax.numpy as jnp

    def _L0_gnn_ref(x, W, U, w_scale):
        import jax, jax.numpy as jnp
        import numpy as np
        B, N, C, R = (4, 2048, 64, 16)
        EPS = 1e-12
        Ws = 0.5 * (W + jnp.swapaxes(W, -1, -2))
        A = jax.nn.sigmoid(U @ U.T)
        K = Ws * A[None, :, :]
        deg = jnp.maximum(K.sum(axis=-1), EPS)
        d = jax.lax.rsqrt(deg)
        K = K * d[:, :, None] * d[:, None, :]
        return w_scale * jnp.einsum('bnm,bmc->bnc', K, x)

    def _L1_gnn_ref(nodes, edges):
        import jax, jax.numpy as jnp
        import numpy as np
        N = nodes.shape[1]
        A = edges + jnp.eye(N, dtype=edges.dtype)
        num = jnp.einsum('bij,bjd->bid', A, nodes)
        denom = jnp.sum(A, axis=2, keepdims=True)
        out = num / denom
        return jnp.where(jnp.isnan(out), jnp.zeros_like(out), out)
    x = _layernorm(x + _L0_gnn_ref(x, adj, L0_gnn_U, L0_gnn_w_scale), axis=-1)
    x = _layernorm(x + _L1_gnn_ref(x, adj), axis=-1)
    return x

_drawn_inputs = setup_inputs


def setup_inputs(seed=0):
    import zlib

    import numpy as np

    out = dict(_drawn_inputs(seed))
    spreads = {}
    factors = {'L0_gnn_U': 64.0}
    for name, (base, spread) in spreads.items():
        noise = np.random.default_rng([zlib.crc32(name.encode()), seed]).standard_normal(out[name].shape)
        drawn = base * np.exp(spread * noise) if base else spread * noise
        out[name] = jnp.asarray(drawn.astype(out[name].dtype))
    for name, factor in factors.items():
        out[name] = (out[name] * factor).astype(out[name].dtype)
    return out
```

```python
from contextlib import ExitStack

import concourse.bass as bass
from concourse import mybir

ALU = mybir.AluOpType
ACT = mybir.ActivationFunctionType
F32 = mybir.dt.float32
BF16 = mybir.dt.bfloat16
AX = mybir.AxisListType

P = 128
B, N, C = 8, 2048, 64
R = 16
NB = N // P
G = 4
NG = NB // G
SW = G * P
EPS_DEG = 1e-12
EPS_LN = 1e-5
TERMS = 8
H, M, L = 0, 1, 2
STAT_PARTS = (H, M, H, M, L, H, L, M)
MOVE_PARTS = (H, H, M, M, H, L, M, L)

STRIPS = [(j, i, r) for j in range(NG) for i in range(j + 1) for r in range(G)]
NS = len(STRIPS)
STRIP_NO = {s: n for n, s in enumerate(STRIPS)}
SUPERS = [(i, j) for i in range(NG) for j in reversed(range(i, NG))]
TURNS = [(i, j, r) for i, j in SUPERS for r in range(G) if not (i == j and r == G - 1)]
NT = len(TURNS)
TURN_NO = {s: n for n, s in enumerate(TURNS)}

K_AT = {}
_at = 0
for _i, _j in SUPERS:
    for _r in range(G):
        K_AT[(_i, _j, _r)] = _at
        _at += SW if _i != _j else SW - P * _r
K_COLS = _at


def build(nc, x, adj, u, w_scale, out, u_scratch):
    with ExitStack() as ctx:
        def sb(name, shape, dt=F32):
            return ctx.enter_context(nc.sbuf_tensor(name, shape, dt))

        def sem(name):
            return ctx.enter_context(nc.semaphore(name))

        w_sb = sb("w_sb", [P, NB, N])
        k_sb = sb("k_sb", [P, K_COLS])
        z_sb = sb("z_sb", [P, NB, C])
        u_stat = sb("u_stat", [P, N], BF16)
        u_move = sb("u_move", [P, SW], BF16)
        colsum_sb = sb("colsum_sb", [P, SW // 2])
        ident = sb("ident", [P, P])
        fold = sb("fold", [P, C])
        ones = sb("ones", [P, 32])
        pick = sb("pick", [P, 1])
        row_parts = sb("row_parts", [P, NB, NG])
        deg = sb("deg", [P, NB])
        d_sb = sb("d_sb", [P, NB])
        scaled_d = sb("scaled_d", [P, NB])
        w_low = sb("w_low", [P, NB])
        w_up = sb("w_up", [P, NB])
        denom = sb("denom", [P, NB])
        scale_sb = sb("scale_sb", [P, 1])
        minus_half = sb("minus_half", [P, NB])
        mean = sb("mean", [P, 2, G])
        var = sb("var", [P, 2, G])
        rstd = sb("rstd", [P, 2, G])

        acc = [ctx.enter_context(nc.psum_tensor(f"acc{c}", [P, SW], F32)) for c in range(NG)]
        ps_w = [ctx.enter_context(nc.psum_tensor(f"ps_w{i}", [P, SW], F32)) for i in range(2)]
        ps_a = [ctx.enter_context(nc.psum_tensor(f"ps_a{i}", [P, SW], F32)) for i in range(2)]

        x_res = k_sb[:, 0:NB * C].rearrange("p (n c) -> p n c", c=C)
        y_sb = k_sb[:, NB * C:NB * C + SW]
        t_sb = [k_sb[:, NB * C + SW + i * G * C:NB * C + SW + (i + 1) * G * C].rearrange("p (n c) -> p n c", c=C)
                for i in range(2)]

        def in_w(row, cols, dt=F32):
            ap = w_sb[:, row, 0:cols]
            return ap if dt == F32 else ap.bitcast(dt)

        u_nat = in_w(12, NB * R).rearrange("p (n r) -> p n r", r=R)
        u_rest = w_sb[:, 12, 512:512 + NB * R].rearrange("p (n r) -> p n r", r=R)
        u_part = [w_sb[:, 12, 1024 + 128 * i:1024 + 128 * (i + 1)].bitcast(BF16).rearrange("p (n r) -> p n r", r=R)
                  for i in range(3)]
        ident_b = w_sb[:, 12, 1536:1600].bitcast(BF16)
        cat_stat = in_w(13, NB * P // 2, BF16).rearrange("p (n g r) -> p n g r", g=TERMS, r=R)
        cat_move = in_w(14, NB * P // 2, BF16).rearrange("p (n g r) -> p n g r", g=TERMS, r=R)
        move_all = in_w(15, N // 2, BF16)

        small_in = sem("small_in")
        ident_made = sem("ident_made")
        const_made = sem("const_made")
        u_split = sem("u_split")
        u_turned = sem("u_turned")
        u_kept = sem("u_kept")
        u_stored = sem("u_stored")
        w_in = [sem(f"w_in{j}") for j in range(NG)]
        move_in = sem("move_in")
        z_in = sem("z_in")
        xres_in = sem("xres_in")
        out_stored = sem("out_stored")
        low_summed = sem("low_summed")
        v_ready = sem("v_ready")
        gate_ready = sem("gate_ready")
        wt_ready = sem("wt_ready")
        s_ready = sem("s_ready")
        wt_kept = sem("wt_kept")
        k_ready = sem("k_ready")
        acc0_zero = sem("acc0_zero")
        col_ready = sem("col_ready")
        col_out = sem("col_out")
        col_turned = sem("col_turned")
        deg_step = sem("deg_step")
        d_ready = sem("d_ready")
        z_ready = sem("z_ready")
        used_straight = sem("used_straight")
        kt_ready = sem("kt_ready")
        kt_kept = sem("kt_kept")
        up_summed = sem("up_summed")
        wu_ready = sem("wu_ready")
        wu_kept = sem("wu_kept")
        scratch_free = sem("scratch_free")
        y_ready = sem("y_ready")
        y_out = [sem(f"y_out{i}") for i in (1, 2)]
        yn_ready = [sem(f"yn_ready{i}") for i in (1, 2)]
        ln_step = [sem(f"ln_step{i}") for i in (1, 2)]
        var_ready = [sem(f"var_ready{i}") for i in (1, 2)]
        rstd_ready = [sem(f"rstd_ready{i}") for i in (1, 2)]
        ln_ready = [sem(f"ln_ready{i}") for i in (1, 2)]
        den_step = sem("den_step")
        freed = sem("freed")

        adj_v = adj.rearrange("b (n p) m -> b p n m", p=P)
        x_v = x.rearrange("b (n p) c -> b p n c", p=P)
        out_v = out.rearrange("b (n p) c -> b p n c", p=P)

        def first_col(i, j, r):
            return i * G + r if i == j else j * G

        def k_strip(i, j, r):
            w = (SW - P * r) if i == j else SW
            at = K_AT[(i, j, r)]
            return k_sb[:, at:at + w]

        def turned_cols(i, j, r):
            return (i * G + r + 1, G - 1 - r) if i == j else (j * G, G)

        def k_turned(i, j, r):
            w = turned_cols(i, j, r)[1] * P
            at = K_AT[(i, j, r)] + (P if i == j else 0)
            return k_sb[:, at:at + w]

        def pe_setup(pe):
            pe.wait_ge(u_split, 6 + 2 * TERMS)
            for n in range(2 * NB):
                if n >= 2:
                    pe.wait_ge(u_kept, n - 1)
                cat = (cat_stat if n < NB else cat_move)[:, n % NB, :, :].rearrange("p g r -> p (g r)")
                pe.matmul(ps_w[n % 2][:, 0:P], cat, ident_b, start=True, stop=True).then_inc(u_turned, 1)
            pe.wait_ge(u_kept, 2 * NB)

        def pe_p1_strip(pe, b, s):
            j, i, r = STRIPS[s]
            row = i * G + r
            c0 = first_col(i, j, r)
            blocks = (j + 1) * G - c0
            if (i, r) == (0, 0):
                pe.wait_ge(move_in, b * 16 * NG + 16 * (j + 1))
            if s >= 2:
                pe.wait_ge(k_ready, b * NS + s - 1)
            off = (c0 - j * G) * P
            pe.matmul(ps_a[s % 2][:, 0:blocks * P], u_stat[:, row * P:(row + 1) * P], u_move[:, off:SW],
                      start=True, stop=True).then_inc(v_ready, 1)
            if (i, r) == (0, 0):
                pe.wait_ge(low_summed, b * NB + (j + 1) * G)
            if s >= 2:
                pe.wait_ge(wt_kept, b * NS + s - 1)
            for q in range(blocks):
                t = pe.transpose(ps_w[s % 2][:, q * P:(q + 1) * P],
                                 w_sb[:, c0 + q, row * P:(row + 1) * P], ident[:, :])
            t.then_inc(wt_ready, 1)

        def pe_colsum(pe, b3, b, j):
            pe.wait_ge(k_ready, b * NS + STRIP_NO[(j, j, G - 1)] + 1)
            if j == 0:
                pe.wait_ge(acc0_zero, b + 1)
            elif b3 is not None:
                pe.wait_ge(var_ready[1], b3 * NG + j + 1)
            for i in range(j + 1):
                for r in range(G if i < j else G - 1):
                    rhs = k_strip(i, j, r) if i < j else k_turned(i, j, r)
                    c = 0 if i < j else (r + 1) * P
                    m = pe.matmul(acc[j][32 * r:32 * r + 32, c:SW], ones[:, :], rhs,
                                  start=(i == 0 and j > 0), stop=True, skip_group_check=True,
                                  tile_position=(0, 32 * r))
            m.then_inc(col_ready, 1)

        def pe_colturn(pe, b, j):
            for h in range(2):
                pe.wait_ge(col_out, b * 2 * NG + 2 * j + h + 1)
                for q in range(2):
                    m = pe.matmul(acc[j][:, 2 * h + q:2 * h + q + 1], colsum_sb[:, q * P:(q + 1) * P], pick[:, :],
                                  start=True, stop=True)
                m.then_inc(col_turned, 1)

        def straight(i, j):
            return [(j, r % 2, i * G + r, k_strip(i, j, r), (P * r if i == j else 0)) for r in range(G)]

        def turned(i, j):
            if i != j:
                at = K_AT[(i, j, 0)]
                quad = k_sb[:, at:at + G * SW].rearrange("p (r m) -> p r m", r=G)
                return [(i, q % 2, j * G + q, quad[:, :, q * P:(q + 1) * P], 0) for q in range(G)]
            found = []
            for r in range(G - 1):
                for q in range(r + 1, G):
                    at = K_AT[(i, i, r)] + (q - r) * P
                    found.append((i, q % 2, i * G + q, k_sb[:, at:at + P], r * P))
            return found

        def pe_products(pe, products, begun):
            for c, half, m, rhs, at in products:
                width = rhs.shape[-1] * (rhs.shape[1] if len(rhs.shape) == 3 else 1)
                mm = pe.matmul(acc[c][64 * half:64 * half + 64, at:at + width], z_sb[:, m, :], rhs,
                               start=(c, half) not in begun, stop=True, skip_group_check=True,
                               tile_position=(0, 64 * half))
                begun.add((c, half))
            return mm

        def pe_turn(pe, b, t):
            i, j, r = TURNS[t]
            c0, blocks = turned_cols(i, j, r)
            if t >= 2:
                pe.wait_ge(kt_kept, b * NT + t - 1)
            for q in range(blocks):
                m = pe.transpose(ps_a[t % 2][:, q * P:(q + 1) * P], k_turned(i, j, r)[:, q * P:(q + 1) * P], ident[:, :])
            m.then_inc(kt_ready, 1)
            if t >= 2:
                pe.wait_ge(wu_kept, b * NT + t - 1)
            for q in range(blocks):
                m = pe.transpose(ps_w[t % 2][:, q * P:(q + 1) * P], w_sb[:, i * G + r, (c0 + q) * P:(c0 + q + 1) * P],
                                 ident[:, :])
            m.then_inc(wu_ready, 1)

        def pe_yn(pe, b, ln, c):
            pe.wait_ge(y_out[ln], b * NG + c + 1)
            for q in range(G):
                m = pe.matmul(acc[c][:, q * C:(q + 1) * C], y_sb[:, q * P:(q + 1) * P], fold[:, :],
                              start=True, stop=True)
            m.then_inc(yn_ready[ln], 1)

        def pe_p2(pe, b):
            pe.wait_ge(wt_kept, b * NS + NS)
            pe.wait_ge(z_ready, b + 1)
            begun = set()

            def finish(s):
                i, j = SUPERS[s]
                last = [t for t in range(NT) if TURNS[t][:2] == (i, j)][-1]
                pe.wait_ge(kt_kept, b * NT + last + 1)
                m = pe_products(pe, turned(i, j), begun)
                if s == 0:
                    m.then_inc(scratch_free, 1)
                if i == j:
                    m.then_inc(y_ready, 1)

            for s, (i, j) in enumerate(SUPERS):
                pe_products(pe, straight(i, j), begun).then_inc(used_straight, 1)
                turns = [t for t in range(NT) if TURNS[t][:2] == (i, j)]
                for t in turns[:2]:
                    pe_turn(pe, b, t)
                if s > 0:
                    finish(s - 1)
                for t in turns[2:]:
                    pe_turn(pe, b, t)
            finish(len(SUPERS) - 1)
            for c in range(NG):
                pe_yn(pe, b, 0, c)

        def p3_products(k):
            pairs = [(m, c) for c in range(k + 1) for m in range(k * G, (k + 1) * G)]
            pairs += [(m, k) for m in range(k * G)]
            return [(c, m % 2, m, w_sb[:, c * G:(c + 1) * G, m * P:(m + 1) * P], 0) for m, c in pairs]

        def pe_w1(pe, b3, b1):
            begun = set()
            strips = list(range(NS)) if b1 is not None else []
            by_j = [[s for s in strips if STRIPS[s][0] == j] for j in range(NG)]
            if b3 is not None:
                pe.wait_ge(wu_kept, b3 * NT + NT)
                for k in range(NG):
                    pe.wait_ge(ln_ready[0], b3 * NG + k + 1)
                    products = p3_products(k)
                    among = by_j[k - 2] if k >= 2 else []
                    share = -(-len(products) // (len(among) + 1))
                    for n in range(len(among) + 1):
                        part = products[n * share:(n + 1) * share]
                        if part:
                            m = pe_products(pe, part, begun)
                            if (n + 1) * share >= len(products):
                                m.then_inc(freed, 1)
                        if n < len(among):
                            pe_p1_strip(pe, b1, among[n])
                m = None
                for c in range(NG):
                    pe_yn(pe, b3, 1, c)
            if b1 is not None:
                for j in range(NG):
                    if b3 is None or j >= 2:
                        for s in by_j[j]:
                            pe_p1_strip(pe, b1, s)
                    if j == 2:
                        for k in range(3):
                            pe_colsum(pe, b3, b1, k)
                            pe_colturn(pe, b1, k)
                pe_colsum(pe, b3, b1, 3)
                pe_colturn(pe, b1, 3)

        def act_setup(act):
            for n in range(2 * NB):
                act.wait_ge(u_turned, n + 1)
                if n < NB:
                    dst = u_stat[:, n * P:(n + 1) * P]
                else:
                    dst = move_all[:, (n - NB) * P:(n - NB + 1) * P]
                act.activation(dst, ps_w[n % 2][:, 0:P], ACT.Copy).then_inc(u_kept, 1)

        def act_row_sums(act, b, j):
            act.wait_ge(w_in[j], b * (16 if j == 0 else 32) + (16 if j == 0 else 32))
            for n in range(j * G, (j + 1) * G):
                row = w_sb[:, n, 0:(j + 1) * SW]
                act.activation(row, row, ACT.Copy, accum_out=w_low[:, n:n + 1]).then_inc(low_summed, 1)

        def act_gate(act, b, s):
            j, i, r = STRIPS[s]
            w = ((j + 1) * G - first_col(i, j, r)) * P
            act.wait_ge(v_ready, b * NS + s + 1)
            act.activation(ps_a[s % 2][:, 0:w], ps_a[s % 2][:, 0:w], ACT.Sigmoid).then_inc(gate_ready, 1)

        def act_keep_wt(act, b, s):
            j, i, r = STRIPS[s]
            c0, row = first_col(i, j, r), i * G + r
            blocks = (j + 1) * G - c0
            act.wait_ge(s_ready, b * NS + s + 1)
            act.activation(w_sb[:, c0:c0 + blocks, row * P:(row + 1) * P],
                           ps_w[s % 2][:, 0:blocks * P].rearrange("p (q m) -> p q m", q=blocks),
                           ACT.Copy).then_inc(wt_kept, 1)

        def act_p1(act, b, js):
            for j in js:
                mine = [s for s in range(NS) if STRIPS[s][0] == j]
                act_row_sums(act, b, j)
                act_gate(act, b, mine[0])
                for s in mine:
                    if s + 1 in mine:
                        act_gate(act, b, s + 1)
                    act_keep_wt(act, b, s)

        def act_y_out(act, b, ln, c):
            if ln == 0:
                act.wait_ge(y_ready, b * NG + c + 1)
            else:
                act.wait_ge(freed, b * NG + NG)
            if c > 0:
                act.wait_ge(yn_ready[ln], b * NG + c)
            act.activation(y_sb, acc[c][:, :], ACT.Copy).then_inc(y_out[ln], 1)

        def act_p2(act, b):
            for t, (i, j, r) in enumerate(TURNS):
                act.wait_ge(used_straight, b * len(SUPERS) + SUPERS.index((i, j)) + 1)
                act.wait_ge(kt_ready, b * NT + t + 1)
                w = turned_cols(i, j, r)[1] * P
                act.activation(k_turned(i, j, r), ps_a[t % 2][:, 0:w], ACT.Copy).then_inc(kt_kept, 1)
            act.wait_ge(scratch_free, b + 1)
            for c in range(NG):
                act_y_out(act, b, 0, c)

        def act_w1(act, b3, b1):
            if b3 is not None:
                if b1 is not None:
                    act_p1(act, b1, (0, 1))
                for c in range(NG):
                    act_y_out(act, b3, 1, c)
                if b1 is not None:
                    act_p1(act, b1, (2, 3))
            else:
                act_p1(act, b1, range(NG))

        def dve_setup(v):
            v.memset(ones[:, :], 1.0).then_inc(const_made, 1)
            v.memset(pick[:, :], 0.0).then_inc(const_made, 1)
            v.memset(row_parts[:, :, :], 0.0).then_inc(const_made, 1)
            v.memset(w_up[:, :], 0.0).then_inc(const_made, 1)
            v.memset(minus_half[:, :], -0.5).then_inc(const_made, 1)
            v.wait_ge(const_made, 2)
            for g in range(4):
                v.memset(pick[32 * g:32 * g + 1, :], 1.0).then_inc(const_made, 1)
            v.wait_ge(ident_made, 2)
            v.wait_ge(small_in, 32)
            v.tensor_copy(ident_b, ident[:, :]).then_inc(u_split, 1)
            v.tensor_tensor(fold[:, :], ident[:, 0:C], ident[:, C:P], ALU.add).then_inc(const_made, 1)
            v.tensor_copy(u_part[H], u_nat).then_inc(u_split, 1)
            v.wait_ge(u_split, 2)
            v.tensor_tensor(u_rest, u_nat, u_part[H], ALU.subtract).then_inc(u_split, 1)
            v.wait_ge(u_split, 3)
            v.tensor_copy(u_part[M], u_rest).then_inc(u_split, 1)
            v.wait_ge(u_split, 4)
            v.tensor_tensor(u_nat, u_rest, u_part[M], ALU.subtract).then_inc(u_split, 1)
            v.wait_ge(u_split, 5)
            v.tensor_copy(u_part[L], u_nat).then_inc(u_split, 1)
            v.wait_ge(u_split, 6)
            for g in range(TERMS):
                v.tensor_copy(cat_stat[:, :, g, :], u_part[STAT_PARTS[g]]).then_inc(u_split, 1)
                v.tensor_copy(cat_move[:, :, g, :], u_part[MOVE_PARTS[g]]).then_inc(u_split, 1)

        def dve_p1_strip(v, b, s):
            j, i, r = STRIPS[s]
            c0, row = first_col(i, j, r), i * G + r
            blocks = (j + 1) * G - c0
            dst = k_strip(i, j, r)
            v.wait_ge(wt_ready, b * NS + s + 1)
            v.tensor_tensor(dst, w_sb[:, row, c0 * P:(c0 + blocks) * P], ps_w[s % 2][:, 0:blocks * P],
                            ALU.add).then_inc(s_ready, 1)
            v.wait_ge(s_ready, b * NS + s + 1)
            v.wait_ge(gate_ready, b * NS + s + 1)
            v.scalar_tensor_tensor(out=dst, in0=dst, scalar=0.5, in1=ps_a[s % 2][:, 0:blocks * P],
                                   op0=ALU.mult, op1=ALU.mult,
                                   accum_out=row_parts[:, row, j:j + 1]).then_inc(k_ready, 1)

        def dve_degrees(v, b, js):
            for j in js:
                for h in range(2):
                    if h == 0:
                        v.wait_ge(col_ready, b * NG + j + 1)
                        if j > 0:
                            v.wait_ge(col_turned, b * 2 * NG + 2 * j)
                    else:
                        v.wait_ge(col_turned, b * 2 * NG + 2 * j + 1)
                    v.tensor_copy(colsum_sb[:, :], acc[j][:, h * SW // 2:(h + 1) * SW // 2]).then_inc(col_out, 1)
                v.wait_ge(col_turned, b * 2 * NG + 2 * j + 2)
                v.tensor_copy(deg[:, j * G:(j + 1) * G], acc[j][:, 0:G]).then_inc(deg_step, 1)

        def dve_z(v, b):
            v.wait_ge(k_ready, b * NS + NS)
            v.tensor_reduce(denom[:, :], row_parts[:, :, :], AX.X, ALU.add).then_inc(deg_step, 1)
            v.wait_ge(deg_step, b * 8 + 5)
            v.tensor_tensor(deg[:, :], deg[:, :], denom[:, :], ALU.add).then_inc(deg_step, 1)
            v.wait_ge(deg_step, b * 8 + 6)
            v.tensor_scalar(deg[:, :], deg[:, :], EPS_DEG, None, ALU.max).then_inc(deg_step, 1)
            v.wait_ge(d_ready, b + 1)
            v.wait_ge(z_in, b * 16 + 16)
            v.tensor_scalar(scaled_d[:, :], d_sb[:, :], scale_sb[:, 0:1], None, ALU.mult).then_inc(deg_step, 1)
            v.tensor_tensor(z_sb[:, :, :], z_sb[:, :, :], d_sb[:, :].unsqueeze(2).to_broadcast([P, NB, C]),
                            ALU.mult).then_inc(z_ready, 1)

        def dve_p2(v, b):
            for t, (i, j, r) in enumerate(TURNS):
                c0, blocks = turned_cols(i, j, r)
                row = i * G + r
                if j == NG - 1 and i < NG - 1:
                    v.tensor_reduce(w_up[:, row:row + 1], w_sb[:, row, (i + 1) * SW:N], AX.X,
                                    ALU.add).then_inc(up_summed, 1)
                    v.wait_ge(up_summed, b * (NB - G + 1) + row + 1)
                v.wait_ge(wu_ready, b * NT + t + 1)
                v.tensor_copy(w_sb[:, row, c0 * P:(c0 + blocks) * P], ps_w[t % 2][:, 0:blocks * P]).then_inc(wu_kept, 1)
            v.tensor_tensor(denom[:, :], w_low[:, :], w_up[:, :], ALU.add).then_inc(up_summed, 1)

        def chunk(ap, c):
            return ap[:, c * G:(c + 1) * G, :]

        def wide(ap):
            return ap.unsqueeze(2).to_broadcast([P, G, C])

        LN_STEPS = (7, 10)

        def dve_ln_center(v, b, ln, c):
            t, mu, sq = t_sb[c % 2], mean[:, c % 2, :], acc[c][:, G * C:2 * G * C].rearrange("p (n c) -> p n c", c=C)
            yn = acc[c][:, 0:G * C].rearrange("p (n c) -> p n c", c=C)
            step = ln_step[ln]
            done = (b * NG + c) * LN_STEPS[ln]
            v.wait_ge(yn_ready[ln], b * NG + c + 1)
            if ln == 0:
                v.tensor_tensor(t, yn, wide(scaled_d[:, c * G:(c + 1) * G]), ALU.mult).then_inc(step, 1)
                if c == 0:
                    v.wait_ge(xres_in, b * 16 + 16)
                v.wait_ge(step, done + 1)
                v.tensor_tensor(t, t, chunk(x_res, c), ALU.add).then_inc(step, 1)
                done = done + 2
            else:
                v.tensor_tensor(t, yn, chunk(z_sb, c), ALU.add).then_inc(step, 1)
                v.wait_ge(step, done + 1)
                v.tensor_tensor(t, t, wide(denom[:, c * G:(c + 1) * G]), ALU.mult).then_inc(step, 1)
                v.wait_ge(step, done + 2)
                v.tensor_scalar(sq, t, 0.0, None, ALU.max).then_inc(step, 1)
                v.wait_ge(step, done + 3)
                v.scalar_tensor_tensor(out=t, in0=t, scalar=0.0, in1=sq, op0=ALU.min, op1=ALU.add).then_inc(step, 1)
                v.wait_ge(step, done + 4)
                v.tensor_tensor(t, t, chunk(z_sb, c), ALU.add).then_inc(step, 1)
                done = done + 5
            v.wait_ge(step, done)
            v.tensor_reduce(mu, t, AX.X, ALU.add).then_inc(step, 1)
            v.wait_ge(step, done + 1)
            v.tensor_scalar(mu, mu, 1.0 / C, None, ALU.mult).then_inc(step, 1)
            v.wait_ge(step, done + 2)
            v.tensor_tensor(t, t, wide(mu), ALU.subtract).then_inc(step, 1)
            v.wait_ge(step, done + 3)
            v.tensor_tensor(sq, t, t, ALU.mult).then_inc(step, 1)
            v.wait_ge(step, done + 4)
            v.tensor_reduce(var[:, c % 2, :], sq, AX.X, ALU.add).then_inc(step, 1)
            v.wait_ge(step, done + 5)
            v.tensor_scalar(var[:, c % 2, :], var[:, c % 2, :], 1.0 / C, EPS_LN, ALU.mult, ALU.add)\
             .then_inc(var_ready[ln], 1)
            if ln == 1 and c == 0:
                v.memset(acc[0][:, :], 0.0).then_inc(acc0_zero, 1)

        def dve_ln_scale(v, b, ln, c):
            v.wait_ge(rstd_ready[ln], b * NG + c + 1)
            dst = chunk(z_sb if ln == 0 else x_res, c)
            v.tensor_tensor(dst, t_sb[c % 2], wide(rstd[:, c % 2, :]), ALU.mult).then_inc(ln_ready[ln], 1)

        def dve_ln(v, b, ln):
            for c in range(NG):
                if c >= 2:
                    dve_ln_scale(v, b, ln, c - 2)
                    v.wait_ge(ln_ready[ln], b * NG + c - 1)
                dve_ln_center(v, b, ln, c)
            dve_ln_scale(v, b, ln, NG - 2)
            dve_ln_scale(v, b, ln, NG - 1)

        def dve_denominator(v, b):
            v.wait_ge(up_summed, b * (NB - G + 1) + NB - G + 1)
            v.tensor_scalar(denom[:, :], denom[:, :], 1.0, None, ALU.add).then_inc(den_step, 1)
            v.wait_ge(den_step, b * 2 + 1)
            v.reciprocal(denom[:, :], denom[:, :]).then_inc(den_step, 1)
            v.wait_ge(den_step, b * 2 + 2)

        def dve_w1(v, b3, b1):
            if b1 is not None and b3 is not None:
                for s in range(STRIP_NO[(2, 0, 0)]):
                    dve_p1_strip(v, b1, s)
            if b3 is not None:
                dve_denominator(v, b3)
                dve_ln(v, b3, 1)
            if b1 is not None:
                if b3 is None:
                    v.memset(acc[0][:, :], 0.0).then_inc(acc0_zero, 1)
                for s in range(0 if b3 is None else STRIP_NO[(2, 0, 0)], NS):
                    if s == STRIP_NO[(3, 0, 0)]:
                        dve_degrees(v, b1, (0, 1, 2))
                        if b3 is not None:
                            v.wait_ge(out_stored, b3 * 16 + 16)
                    dve_p1_strip(v, b1, s)
                dve_degrees(v, b1, (3,))
                dve_z(v, b1)

        def pool_setup(g):
            g.memset(ident[:, :], 1.0).then_inc(ident_made, 1)
            g.wait_ge(ident_made, 1)
            g.affine_select(ident[:, :], ident[:, :], pattern=[[1, P]], compare_op=ALU.is_equal, fill=0.0,
                            base=0, channel_multiplier=-1).then_inc(ident_made, 1)

        def pool_d(g, b):
            g.wait_ge(deg_step, b * 8 + 7)
            g.tensor_tensor(d_sb[:, :], deg[:, :], minus_half[:, :], ALU.pow).then_inc(d_ready, 1)

        def pool_rstd(g, b, ln):
            for c in range(NG):
                g.wait_ge(var_ready[ln], b * NG + c + 1)
                if c >= 2:
                    g.wait_ge(ln_ready[ln], b * NG + c - 1)
                g.tensor_tensor(rstd[:, c % 2, :], var[:, c % 2, :], minus_half[:, 0:G],
                                ALU.pow).then_inc(rstd_ready[ln], 1)

        def sp_w(sp, b, j):
            sp.dma_start(w_sb[:, j * G:(j + 1) * G, 0:(j + 1) * SW],
                         adj_v[b, :, j * G:(j + 1) * G, 0:(j + 1) * SW]).then_inc(w_in[j], 16)
            if j > 0:
                sp.dma_start(w_sb[:, 0:j * G, j * SW:(j + 1) * SW],
                             adj_v[b, :, 0:j * G, j * SW:(j + 1) * SW]).then_inc(w_in[j], 16)

        def sp_move(sp, b, j):
            if j > 0:
                sp.wait_ge(v_ready, b * NS + STRIP_NO[(j, 0, 0)])
            sp.dma_start(u_move[:, :], u_scratch[:, j * SW:(j + 1) * SW]).then_inc(move_in, 16)

        def sp_w1(sp, b3, b1):
            if b3 is None:
                for j in range(NG - 1):
                    sp_w(sp, b1, j)
                sp.wait_ge(u_kept, 2 * NB)
                sp.dma_start(u_scratch[:, :], move_all).then_inc(u_stored, 16)
                sp.wait_ge(u_stored, 16)
                sp_w(sp, b1, NG - 1)
                sp.dma_start(z_sb[:, :, :], x_v[b1, :, :, :]).then_inc(z_in, 16)
                for j in range(NG):
                    sp_move(sp, b1, j)
                return
            for j in range(NG):
                if b1 is not None:
                    sp.wait_ge(freed, b3 * NG + j + 1)
                    sp_w(sp, b1, j)
                    if j >= 1:
                        sp_move(sp, b1, j - 1)
            sp.wait_ge(ln_ready[1], b3 * NG + NG)
            sp.dma_start(out_v[b3, :, :, :], x_res).then_inc(out_stored, 16)
            if b1 is not None:
                sp.dma_start(z_sb[:, :, :], x_v[b1, :, :, :]).then_inc(z_in, 16)
                sp_move(sp, b1, NG - 1)

        def sp_p2(sp, b):
            sp.wait_ge(scratch_free, b + 1)
            sp.dma_start(x_res, x_v[b, :, :, :]).then_inc(xres_in, 16)

        block = ctx.enter_context(nc.Block())

        @block.tensor
        def _(pe):
            pe_setup(pe)
            pe.wait_ge(const_made, 10)
            pe.wait_ge(ident_made, 2)
            pe_w1(pe, None, 0)
            pe_p2(pe, 0)
            with pe.Fori(0, B - 1, 1) as b:
                pe_w1(pe, b, b + 1)
                pe_p2(pe, b + 1)
            pe_w1(pe, B - 1, None)

        @block.scalar
        def _(act):
            act_setup(act)
            act_w1(act, None, 0)
            act_p2(act, 0)
            with act.Fori(0, B - 1, 1) as b:
                act_w1(act, b, b + 1)
                act_p2(act, b + 1)
            act_w1(act, B - 1, None)

        @block.vector
        def _(v):
            dve_setup(v)
            dve_w1(v, None, 0)
            dve_p2(v, 0)
            dve_ln(v, 0, 0)
            with v.Fori(0, B - 1, 1) as b:
                dve_w1(v, b, b + 1)
                dve_p2(v, b + 1)
                dve_ln(v, b + 1, 0)
            dve_w1(v, B - 1, None)

        @block.gpsimd
        def _(g):
            pool_setup(g)
            pool_d(g, 0)
            pool_rstd(g, 0, 0)
            with g.Fori(0, B - 1, 1) as b:
                pool_rstd(g, b, 1)
                pool_d(g, b + 1)
                pool_rstd(g, b + 1, 0)
            pool_rstd(g, B - 1, 1)

        @block.sync
        def _(sp):
            sp.dma_start(u_nat, u.rearrange("(n p) r -> p n r", p=P)).then_inc(small_in, 16)
            sp.dma_start(scale_sb[:, :], w_scale.to_broadcast([P, 1])).then_inc(small_in, 16)
            sp_w1(sp, None, 0)
            sp_p2(sp, 0)
            with sp.Fori(0, B - 1, 1) as b:
                sp_w1(sp, b, b + 1)
                sp_p2(sp, b + 1)
            sp_w1(sp, B - 1, None)
            sp.wait_ge(out_stored, 16 * B)


def kernel(**inputs):
    import numpy as _np
    import concourse.bacc as _bacc
    from concourse import mybir as _mybir
    from concourse.bass_utils import run_bass_kernel_spmd as _run

    nc = _bacc.Bacc("TRN2", target_bir_lowering=False, num_devices=1)
    arrays, args = {}, []
    for name in ("x", "adj", "L0_gnn_U", "L0_gnn_w_scale"):
        a = _np.ascontiguousarray(inputs[name])
        if name == "L0_gnn_w_scale":
            a = a.reshape(1, 1)
        arrays[f"in_{name}"] = a
        args.append(nc.dram_tensor(f"in_{name}", a.shape, _mybir.dt.from_np(a.dtype), kind="ExternalInput").ap())
    args.append(nc.dram_tensor("out_x", (B, N, C), F32, kind="ExternalOutput").ap())
    args.append(nc.dram_tensor("u_scratch", (P, N), BF16, kind="Internal").ap())
    build(nc, *args)
    r = _run(nc, [arrays], core_ids=[0])
    return r.results[0]["out_x"]
```

```python
from contextlib import ExitStack

import concourse.bass as bass
from concourse import mybir

ALU = mybir.AluOpType
ACT = mybir.ActivationFunctionType
F32 = mybir.dt.float32
BF16 = mybir.dt.bfloat16
AX = mybir.AxisListType

P = 128
B, N, C = 8, 2048, 64
R = 16
NB = N // P
G = 4
NG = NB // G
SW = G * P
EPS_DEG = 1e-12
EPS_LN = 1e-5
TERMS = 8
H, M, L = 0, 1, 2
STAT_PARTS = (H, M, H, M, L, H, L, M)
MOVE_PARTS = (H, H, M, M, H, L, M, L)

STRIPS = [(j, i, r) for j in range(NG) for i in range(j + 1) for r in range(G)]
NS = len(STRIPS)
STRIP_NO = {s: n for n, s in enumerate(STRIPS)}
SUMS_AFTER = {}
for _j in range(NG):
    for _i in range(_j + 1):
        _s = STRIP_NO[(_j, _i, G - 1)] + 2
        if _j == 0:
            _s = STRIP_NO[(2, 0, 2)]
        if _j == 1:
            _s = STRIP_NO[(2, 0, 3)] + 2 * _i
        if _j == NG - 1 == _i:
            continue
        SUMS_AFTER.setdefault(_s, []).append((_i, _j))
DEGREES_AFTER = [STRIP_NO[(3, 0, 0)], STRIP_NO[(3, 0, 2)], STRIP_NO[(3, 1, 0)]]
SUPERS = [(i, j) for i in range(NG) for j in reversed(range(i, NG))]
TURNS = [(i, j, r) for i, j in SUPERS for r in range(G) if not (i == j and r == G - 1)]
NT = len(TURNS)
LAST_TURN = {(i, j): n for n, (i, j, r) in enumerate(TURNS)}

K_AT = {}
_at = 0
for _i, _j in SUPERS:
    for _r in range(G):
        K_AT[(_i, _j, _r)] = _at
        _at += SW if _i != _j else SW - P * _r
K_COLS = _at
COL_OUTS = 2 * (NG - 1) + 1


def build(nc, x, adj, u, w_scale, out, u_scratch):
    with ExitStack() as ctx:
        def sb(name, shape, dt=F32):
            return ctx.enter_context(nc.sbuf_tensor(name, shape, dt))

        def sem(name):
            return ctx.enter_context(nc.semaphore(name))

        w_sb = sb("w_sb", [P, NB, N])
        k_sb = sb("k_sb", [P, K_COLS])
        z_sb = sb("z_sb", [P, NB, C])
        u_stat = sb("u_stat", [P, N], BF16)
        colsum_sb = sb("colsum_sb", [P, SW])
        u_move = [colsum_sb[:, i * SW // 2:(i + 1) * SW // 2].bitcast(BF16) for i in range(2)]
        ident = sb("ident", [P, P])
        fold = sb("fold", [P, C])
        ones = sb("ones", [P, 32])
        pick = sb("pick", [P, 1])
        row_parts = sb("row_parts", [P, NB, NG])
        deg = sb("deg", [P, NB])
        d_sb = sb("d_sb", [P, NB])
        scaled_d = sb("scaled_d", [P, NB])
        w_low = sb("w_low", [P, NB])
        w_up = sb("w_up", [P, NB])
        denom = sb("denom", [P, NB])
        scale_sb = sb("scale_sb", [P, 1])
        minus_half = sb("minus_half", [P, NB])
        mean = sb("mean", [P, 2, G])
        var = sb("var", [P, 2, G])
        rstd = sb("rstd", [P, 2, G])

        acc = [ctx.enter_context(nc.psum_tensor(f"acc{c}", [P, SW], F32)) for c in range(NG)]
        ps_w = [ctx.enter_context(nc.psum_tensor(f"ps_w{i}", [P, SW], F32)) for i in range(2)]
        ps_a = [ctx.enter_context(nc.psum_tensor(f"ps_a{i}", [P, SW], F32)) for i in range(2)]

        x_res = k_sb[:, 0:NB * C].rearrange("p (n c) -> p n c", c=C)
        y_sb = k_sb[:, NB * C:NB * C + SW]
        t_sb = [k_sb[:, NB * C + SW + i * G * C:NB * C + SW + (i + 1) * G * C].rearrange("p (n c) -> p n c", c=C)
                for i in range(2)]

        def in_w(row, cols, dt=F32):
            ap = w_sb[:, row, 0:cols]
            return ap if dt == F32 else ap.bitcast(dt)

        u_nat = in_w(12, NB * R).rearrange("p (n r) -> p n r", r=R)
        u_rest = w_sb[:, 12, 512:512 + NB * R].rearrange("p (n r) -> p n r", r=R)
        u_part = [w_sb[:, 12, 1024 + 128 * i:1024 + 128 * (i + 1)].bitcast(BF16).rearrange("p (n r) -> p n r", r=R)
                  for i in range(3)]
        ident_b = w_sb[:, 12, 1536:1600].bitcast(BF16)
        cat_stat = in_w(13, NB * P // 2, BF16).rearrange("p (n g r) -> p n g r", g=TERMS, r=R)
        cat_move = in_w(14, NB * P // 2, BF16).rearrange("p (n g r) -> p n g r", g=TERMS, r=R)
        move_all = in_w(15, N // 2, BF16)

        small_in = sem("small_in")
        ident_made = sem("ident_made")
        const_made = sem("const_made")
        u_split = sem("u_split")
        u_turned = sem("u_turned")
        u_kept = sem("u_kept")
        u_stored = sem("u_stored")
        w_row = [sem(f"w_row{n}") for n in range(NB)]
        w_col = {(i, j): sem(f"w_col{i}{j}") for j in range(NG) for i in range(j)}
        move_in = [sem(f"move_in{i}") for i in range(2)]
        z_in = sem("z_in")
        xres_in = sem("xres_in")
        out_stored = sem("out_stored")
        low_summed = sem("low_summed")
        v_ready = sem("v_ready")
        gate_ready = sem("gate_ready")
        wt_ready = sem("wt_ready")
        s_ready = sem("s_ready")
        wt_kept = sem("wt_kept")
        k_ready = sem("k_ready")
        acc0_zero = sem("acc0_zero")
        col_ready = sem("col_ready")
        col_out = sem("col_out")
        col_turned = sem("col_turned")
        deg_step = sem("deg_step")
        d_ready = sem("d_ready")
        z_ready = sem("z_ready")
        used_straight = sem("used_straight")
        kt_ready = sem("kt_ready")
        kt_kept = sem("kt_kept")
        up_summed = sem("up_summed")
        wu_ready = sem("wu_ready")
        wu_kept = sem("wu_kept")
        scratch_free = sem("scratch_free")
        y_ready = sem("y_ready")
        y_out = [sem(f"y_out{i}") for i in (1, 2)]
        yn_ready = [sem(f"yn_ready{i}") for i in (1, 2)]
        ln_step = [sem(f"ln_step{i}") for i in (1, 2)]
        var_ready = [sem(f"var_ready{i}") for i in (1, 2)]
        rstd_ready = [sem(f"rstd_ready{i}") for i in (1, 2)]
        ln_ready = [sem(f"ln_ready{i}") for i in (1, 2)]
        den_step = sem("den_step")
        freed = sem("freed")

        adj_v = adj.rearrange("b (n p) m -> b p n m", p=P)
        x_v = x.rearrange("b (n p) c -> b p n c", p=P)
        out_v = out.rearrange("b (n p) c -> b p n c", p=P)

        def first_col(i, j, r):
            return i * G + r if i == j else j * G

        def k_strip(i, j, r):
            w = (SW - P * r) if i == j else SW
            at = K_AT[(i, j, r)]
            return k_sb[:, at:at + w]

        def turned_cols(i, j, r):
            return (i * G + r + 1, G - 1 - r) if i == j else (j * G, G)

        def k_turned(i, j, r):
            w = turned_cols(i, j, r)[1] * P
            at = K_AT[(i, j, r)] + (P if i == j else 0)
            return k_sb[:, at:at + w]

        def pe_setup(pe):
            pe.wait_ge(u_split, 6 + 2 * TERMS)
            for n in range(2 * NB):
                if n >= 2:
                    pe.wait_ge(u_kept, n - 1)
                cat = (cat_stat if n < NB else cat_move)[:, n % NB, :, :].rearrange("p g r -> p (g r)")
                pe.matmul(ps_w[n % 2][:, 0:P], cat, ident_b, start=True, stop=True).then_inc(u_turned, 1)
            pe.wait_ge(u_kept, 2 * NB)

        def pe_p1_strip(pe, b, s):
            j, i, r = STRIPS[s]
            row = i * G + r
            c0 = first_col(i, j, r)
            blocks = (j + 1) * G - c0
            if (i, r) == (0, 0):
                pe.wait_ge(low_summed, b * NB + (j + 1) * G)
            if s >= 2:
                pe.wait_ge(wt_kept, b * NS + s - 1)
            for q in range(blocks):
                t = pe.transpose(ps_w[s % 2][:, q * P:(q + 1) * P],
                                 w_sb[:, c0 + q, row * P:(row + 1) * P], ident[:, :])
            t.then_inc(wt_ready, 1)
            if (i, r) == (0, 0):
                pe.wait_ge(move_in[j % 2], b * 32 + 16 * (j // 2 + 1))
            if s >= 2:
                pe.wait_ge(k_ready, b * NS + s - 1)
            off = (c0 - j * G) * P
            pe.matmul(ps_a[s % 2][:, 0:blocks * P], u_stat[:, row * P:(row + 1) * P], u_move[j % 2][:, off:SW],
                      start=True, stop=True).then_inc(v_ready, 1)

        def pe_colsum(pe, b3, b, i, j):
            rows = G if i < j else G - 1
            pe.wait_ge(k_ready, b * NS + STRIP_NO[(j, i, rows - 1)] + 1)
            if i == 0:
                if j == 0:
                    pe.wait_ge(acc0_zero, b + 1)
                elif b3 is not None:
                    pe.wait_ge(var_ready[1], b3 * NG + j + 1)
            for r in range(rows):
                rhs = k_strip(i, j, r) if i < j else k_turned(i, j, r)
                c = 0 if i < j else (r + 1) * P
                m = pe.matmul(acc[j][32 * r:32 * r + 32, c:SW], ones[:, :], rhs,
                              start=(i == 0 and j > 0), stop=True, skip_group_check=True,
                              tile_position=(0, 32 * r))
            if i == j:
                m.then_inc(col_ready, 1)

        def pe_colturn(pe, b, j):
            parts = 2 if j < NG - 1 else 1
            for h in range(parts):
                pe.wait_ge(col_out, b * COL_OUTS + 2 * j + h + 1)
                for q in range(G // parts):
                    at = h * (G // parts) + q
                    m = pe.matmul(acc[j][:, at:at + 1], colsum_sb[:, q * P:(q + 1) * P], pick[:, :],
                                  start=True, stop=True)
                m.then_inc(col_turned, 1)

        def straight(i, j):
            return [(j, r % 2, i * G + r, k_strip(i, j, r), (P * r if i == j else 0)) for r in range(G)]

        def turned(i, j):
            if i != j:
                at = K_AT[(i, j, 0)]
                quad = k_sb[:, at:at + G * SW].rearrange("p (r m) -> p r m", r=G)
                return [(i, q % 2, j * G + q, quad[:, :, q * P:(q + 1) * P], 0) for q in range(G)]
            found = []
            for r in range(G - 1):
                for q in range(r + 1, G):
                    at = K_AT[(i, i, r)] + (q - r) * P
                    found.append((i, q % 2, i * G + q, k_sb[:, at:at + P], r * P))
            return found

        def pe_products(pe, products, begun):
            for c, half, m, rhs, at in products:
                width = rhs.shape[-1] * (rhs.shape[1] if len(rhs.shape) == 3 else 1)
                mm = pe.matmul(acc[c][64 * half:64 * half + 64, at:at + width], z_sb[:, m, :], rhs,
                               start=(c, half) not in begun, stop=True, skip_group_check=True,
                               tile_position=(0, 64 * half))
                begun.add((c, half))
            return mm

        def pe_turn(pe, b, t):
            i, j, r = TURNS[t]
            c0, blocks = turned_cols(i, j, r)
            if t >= 2:
                pe.wait_ge(kt_kept, b * NT + t - 1)
            for q in range(blocks):
                m = pe.transpose(ps_a[t % 2][:, q * P:(q + 1) * P], k_turned(i, j, r)[:, q * P:(q + 1) * P], ident[:, :])
            m.then_inc(kt_ready, 1)
            if t >= 2:
                pe.wait_ge(wu_kept, b * NT + t - 1)
            for q in range(blocks):
                m = pe.transpose(ps_w[t % 2][:, q * P:(q + 1) * P], w_sb[:, i * G + r, (c0 + q) * P:(c0 + q + 1) * P],
                                 ident[:, :])
            m.then_inc(wu_ready, 1)

        def pe_yn(pe, b, ln, c):
            pe.wait_ge(y_out[ln], b * NG + c + 1)
            for q in range(G):
                m = pe.matmul(acc[c][:, q * C:(q + 1) * C], y_sb[:, q * P:(q + 1) * P], fold[:, :],
                              start=True, stop=True)
            m.then_inc(yn_ready[ln], 1)

        def pe_p2(pe, b):
            pe.wait_ge(wt_kept, b * NS + NS)
            pe.wait_ge(z_ready, b + 1)
            begun = set()

            def finish(s):
                i, j = SUPERS[s]
                pe.wait_ge(kt_kept, b * NT + LAST_TURN[(i, j)] + 1)
                m = pe_products(pe, turned(i, j), begun)
                if s == 0:
                    m.then_inc(scratch_free, 1)
                if i == j:
                    m.then_inc(y_ready, 1)

            for s, (i, j) in enumerate(SUPERS):
                pe_products(pe, straight(i, j), begun).then_inc(used_straight, 1)
                turns = [t for t in range(NT) if TURNS[t][:2] == (i, j)]
                for t in turns[:2]:
                    pe_turn(pe, b, t)
                if s > 0:
                    finish(s - 1)
                for t in turns[2:]:
                    pe_turn(pe, b, t)
                if s > 0 and SUPERS[s - 1] == (i - 1, i - 1):
                    pe_yn(pe, b, 0, i - 1)
            finish(len(SUPERS) - 1)
            pe_yn(pe, b, 0, NG - 1)

        def p3_products(k):
            pairs = [(m, c) for c in range(k + 1) for m in range(k * G, (k + 1) * G)]
            pairs += [(m, k) for m in range(k * G)]
            return [(c, m % 2, m, w_sb[:, c * G:(c + 1) * G, m * P:(m + 1) * P], 0) for m, c in pairs]

        def pe_w1(pe, b3, b1):
            begun = set()
            strips = list(range(NS)) if b1 is not None else []
            by_j = [[s for s in strips if STRIPS[s][0] == j] for j in range(NG)]
            if b3 is not None:
                pe.wait_ge(wu_kept, b3 * NT + NT)
                for k in range(NG):
                    pe.wait_ge(ln_ready[0], b3 * NG + k + 1)
                    products = p3_products(k)
                    among = by_j[k - 2] if k >= 2 else []
                    share = -(-len(products) // (len(among) + 1))
                    for n in range(len(among) + 1):
                        part = products[n * share:(n + 1) * share]
                        if part:
                            m = pe_products(pe, part, begun)
                            if (n + 1) * share >= len(products):
                                m.then_inc(freed, 1)
                        if n < len(among):
                            pe_p1_strip(pe, b1, among[n])
                m = None
                for c in range(NG):
                    pe_yn(pe, b3, 1, c)
            if b1 is not None:
                for s in range(0 if b3 is None else STRIP_NO[(2, 0, 0)], NS):
                    pe_p1_strip(pe, b1, s)
                    if s >= STRIP_NO[(2, 0, 2)]:
                        for i, j in SUMS_AFTER.get(s, ()):
                            pe_colsum(pe, b3, b1, i, j)
                    if s - 1 in DEGREES_AFTER:
                        pe_colturn(pe, b1, DEGREES_AFTER.index(s - 1))
                pe_colsum(pe, b3, b1, NG - 1, NG - 1)
                pe_colturn(pe, b1, NG - 1)

        def act_setup(act):
            for n in range(2 * NB):
                act.wait_ge(u_turned, n + 1)
                if n < NB:
                    dst = u_stat[:, n * P:(n + 1) * P]
                else:
                    dst = move_all[:, (n - NB) * P:(n - NB + 1) * P]
                act.activation(dst, ps_w[n % 2][:, 0:P], ACT.Copy).then_inc(u_kept, 1)

        def act_row_sums(act, b, j):
            for n in range(j * G, (j + 1) * G):
                act.wait_ge(w_row[n], b * 16 + 16)
                row = w_sb[:, n, 0:(j + 1) * SW]
                act.activation(row, row, ACT.Copy, accum_out=w_low[:, n:n + 1]).then_inc(low_summed, 1)

        def act_gate(act, b, s):
            j, i, r = STRIPS[s]
            w = ((j + 1) * G - first_col(i, j, r)) * P
            act.wait_ge(v_ready, b * NS + s + 1)
            act.activation(ps_a[s % 2][:, 0:w], ps_a[s % 2][:, 0:w], ACT.Sigmoid).then_inc(gate_ready, 1)

        def act_keep_wt(act, b, s):
            j, i, r = STRIPS[s]
            c0, row = first_col(i, j, r), i * G + r
            blocks = (j + 1) * G - c0
            act.wait_ge(s_ready, b * NS + s + 1)
            act.activation(w_sb[:, c0:c0 + blocks, row * P:(row + 1) * P],
                           ps_w[s % 2][:, 0:blocks * P].rearrange("p (q m) -> p q m", q=blocks),
                           ACT.Copy).then_inc(wt_kept, 1)

        def act_p1(act, b, js):
            for j in js:
                mine = [s for s in range(NS) if STRIPS[s][0] == j]
                act_row_sums(act, b, j)
                for s in mine:
                    if s > mine[0]:
                        act_keep_wt(act, b, s - 1)
                    act_gate(act, b, s)
                act_keep_wt(act, b, mine[-1])

        def act_y_out(act, b, ln, c):
            if ln == 0:
                act.wait_ge(y_ready, b * NG + c + 1)
            else:
                act.wait_ge(freed, b * NG + NG)
            if c > 0:
                act.wait_ge(yn_ready[ln], b * NG + c)
            act.activation(y_sb, acc[c][:, :], ACT.Copy).then_inc(y_out[ln], 1)

        def act_p2(act, b):
            for t, (i, j, r) in enumerate(TURNS):
                act.wait_ge(used_straight, b * len(SUPERS) + SUPERS.index((i, j)) + 1)
                act.wait_ge(kt_ready, b * NT + t + 1)
                w = turned_cols(i, j, r)[1] * P
                act.activation(k_turned(i, j, r), ps_a[t % 2][:, 0:w], ACT.Copy).then_inc(kt_kept, 1)
                if i > 0 and j == NG - 1 and r == 1:
                    if i == 1:
                        act.wait_ge(scratch_free, b + 1)
                    act_y_out(act, b, 0, i - 1)
            act_y_out(act, b, 0, NG - 1)

        def act_w1(act, b3, b1):
            if b3 is not None:
                if b1 is not None:
                    act_p1(act, b1, (0, 1))
                for c in range(NG):
                    act_y_out(act, b3, 1, c)
                if b1 is not None:
                    act_p1(act, b1, (2, 3))
            else:
                act_p1(act, b1, range(NG))

        def dve_setup(v):
            v.memset(ones[:, :], 1.0).then_inc(const_made, 1)
            v.memset(pick[:, :], 0.0).then_inc(const_made, 1)
            v.memset(row_parts[:, :, :], 0.0).then_inc(const_made, 1)
            v.memset(w_up[:, :], 0.0).then_inc(const_made, 1)
            v.memset(minus_half[:, :], -0.5).then_inc(const_made, 1)
            v.wait_ge(const_made, 2)
            for g in range(4):
                v.memset(pick[32 * g:32 * g + 1, :], 1.0).then_inc(const_made, 1)
            v.wait_ge(ident_made, 2)
            v.wait_ge(small_in, 32)
            v.tensor_copy(ident_b, ident[:, :]).then_inc(u_split, 1)
            v.tensor_tensor(fold[:, :], ident[:, 0:C], ident[:, C:P], ALU.add).then_inc(const_made, 1)
            v.tensor_copy(u_part[H], u_nat).then_inc(u_split, 1)
            v.wait_ge(u_split, 2)
            v.tensor_tensor(u_rest, u_nat, u_part[H], ALU.subtract).then_inc(u_split, 1)
            v.wait_ge(u_split, 3)
            v.tensor_copy(u_part[M], u_rest).then_inc(u_split, 1)
            v.wait_ge(u_split, 4)
            v.tensor_tensor(u_nat, u_rest, u_part[M], ALU.subtract).then_inc(u_split, 1)
            v.wait_ge(u_split, 5)
            v.tensor_copy(u_part[L], u_nat).then_inc(u_split, 1)
            v.wait_ge(u_split, 6)
            for g in range(TERMS):
                v.tensor_copy(cat_stat[:, :, g, :], u_part[STAT_PARTS[g]]).then_inc(u_split, 1)
                v.tensor_copy(cat_move[:, :, g, :], u_part[MOVE_PARTS[g]]).then_inc(u_split, 1)

        def dve_s_strip(v, b, s):
            j, i, r = STRIPS[s]
            c0, row = first_col(i, j, r), i * G + r
            blocks = (j + 1) * G - c0
            if i < j and r == 0:
                v.wait_ge(w_col[(i, j)], b * 16 + 16)
            v.wait_ge(wt_ready, b * NS + s + 1)
            v.tensor_tensor(k_strip(i, j, r), w_sb[:, row, c0 * P:(c0 + blocks) * P], ps_w[s % 2][:, 0:blocks * P],
                            ALU.add).then_inc(s_ready, 1)

        def dve_k_strip(v, b, s):
            j, i, r = STRIPS[s]
            dst = k_strip(i, j, r)
            v.wait_ge(s_ready, b * NS + s + 1)
            v.wait_ge(gate_ready, b * NS + s + 1)
            v.scalar_tensor_tensor(out=dst, in0=dst, scalar=0.5, in1=ps_a[s % 2][:, 0:dst.shape[-1]],
                                   op0=ALU.mult, op1=ALU.mult,
                                   accum_out=row_parts[:, i * G + r, j:j + 1]).then_inc(k_ready, 1)

        def dve_degrees(v, b, j):
            parts = 2 if j < NG - 1 else 1
            for h in range(parts):
                if h == 0:
                    v.wait_ge(col_ready, b * NG + j + 1)
                if h > 0 or j > 0:
                    v.wait_ge(col_turned, b * COL_OUTS + 2 * j + h)
                w = SW // parts
                v.tensor_copy(colsum_sb[:, 0:w], acc[j][:, h * w:(h + 1) * w]).then_inc(col_out, 1)
            v.wait_ge(col_turned, b * COL_OUTS + 2 * j + parts)
            v.tensor_copy(deg[:, j * G:(j + 1) * G], acc[j][:, 0:G]).then_inc(deg_step, 1)

        def dve_z(v, b):
            v.wait_ge(k_ready, b * NS + NS)
            v.tensor_reduce(denom[:, :], row_parts[:, :, :], AX.X, ALU.add).then_inc(deg_step, 1)
            v.wait_ge(deg_step, b * 8 + 5)
            v.tensor_tensor(deg[:, :], deg[:, :], denom[:, :], ALU.add).then_inc(deg_step, 1)
            v.wait_ge(deg_step, b * 8 + 6)
            v.tensor_scalar(deg[:, :], deg[:, :], EPS_DEG, None, ALU.max).then_inc(deg_step, 1)
            v.wait_ge(d_ready, b + 1)
            v.wait_ge(z_in, b * 16 + 16)
            v.tensor_scalar(scaled_d[:, :], d_sb[:, :], scale_sb[:, 0:1], None, ALU.mult).then_inc(deg_step, 1)
            v.tensor_tensor(z_sb[:, :, :], z_sb[:, :, :], d_sb[:, :].unsqueeze(2).to_broadcast([P, NB, C]),
                            ALU.mult).then_inc(z_ready, 1)

        def dve_p2(v, b):
            for t, (i, j, r) in enumerate(TURNS):
                c0, blocks = turned_cols(i, j, r)
                row = i * G + r
                if j == NG - 1 and i < NG - 1:
                    v.tensor_reduce(w_up[:, row:row + 1], w_sb[:, row, (i + 1) * SW:N], AX.X,
                                    ALU.add).then_inc(up_summed, 1)
                    v.wait_ge(up_summed, b * (NB - G + 1) + row + 1)
                v.wait_ge(wu_ready, b * NT + t + 1)
                v.tensor_copy(w_sb[:, row, c0 * P:(c0 + blocks) * P], ps_w[t % 2][:, 0:blocks * P]).then_inc(wu_kept, 1)
                if t == LAST_TURN[(NG - 2, NG - 2)]:
                    v.tensor_tensor(denom[:, :], w_low[:, :], w_up[:, :], ALU.add).then_inc(up_summed, 1)
                if i > 0 and t == LAST_TURN[(i, NG - 1)]:
                    dve_ln_center(v, b, 0, i - 1)
                if 0 < i < NG - 1 and t == LAST_TURN[(i, NG - 1)] + 2:
                    dve_ln_scale(v, b, 0, i - 1)
            dve_ln_scale(v, b, 0, NG - 2)
            dve_ln_center(v, b, 0, NG - 1)
            dve_ln_scale(v, b, 0, NG - 1)

        def chunk(ap, c):
            return ap[:, c * G:(c + 1) * G, :]

        def wide(ap):
            return ap.unsqueeze(2).to_broadcast([P, G, C])

        LN_STEPS = (7, 10)

        def dve_ln_center(v, b, ln, c):
            t, mu, sq = t_sb[c % 2], mean[:, c % 2, :], acc[c][:, G * C:2 * G * C].rearrange("p (n c) -> p n c", c=C)
            yn = acc[c][:, 0:G * C].rearrange("p (n c) -> p n c", c=C)
            step = ln_step[ln]
            done = (b * NG + c) * LN_STEPS[ln]
            v.wait_ge(yn_ready[ln], b * NG + c + 1)
            if ln == 0:
                v.tensor_tensor(t, yn, wide(scaled_d[:, c * G:(c + 1) * G]), ALU.mult).then_inc(step, 1)
                if c == 0:
                    v.wait_ge(xres_in, b * 16 + 16)
                v.wait_ge(step, done + 1)
                v.tensor_tensor(t, t, chunk(x_res, c), ALU.add).then_inc(step, 1)
                done = done + 2
            else:
                v.tensor_tensor(t, yn, chunk(z_sb, c), ALU.add).then_inc(step, 1)
                v.wait_ge(step, done + 1)
                v.tensor_tensor(t, t, wide(denom[:, c * G:(c + 1) * G]), ALU.mult).then_inc(step, 1)
                v.wait_ge(step, done + 2)
                v.tensor_scalar(sq, t, 0.0, None, ALU.max).then_inc(step, 1)
                v.wait_ge(step, done + 3)
                v.scalar_tensor_tensor(out=t, in0=t, scalar=0.0, in1=sq, op0=ALU.min, op1=ALU.add).then_inc(step, 1)
                v.wait_ge(step, done + 4)
                v.tensor_tensor(t, t, chunk(z_sb, c), ALU.add).then_inc(step, 1)
                done = done + 5
            v.wait_ge(step, done)
            v.tensor_reduce(mu, t, AX.X, ALU.add).then_inc(step, 1)
            v.wait_ge(step, done + 1)
            v.tensor_scalar(mu, mu, 1.0 / C, None, ALU.mult).then_inc(step, 1)
            v.wait_ge(step, done + 2)
            v.tensor_tensor(t, t, wide(mu), ALU.subtract).then_inc(step, 1)
            v.wait_ge(step, done + 3)
            v.tensor_tensor(sq, t, t, ALU.mult).then_inc(step, 1)
            v.wait_ge(step, done + 4)
            v.tensor_reduce(var[:, c % 2, :], sq, AX.X, ALU.add).then_inc(step, 1)
            v.wait_ge(step, done + 5)
            v.tensor_scalar(var[:, c % 2, :], var[:, c % 2, :], 1.0 / C, EPS_LN, ALU.mult, ALU.add)\
             .then_inc(var_ready[ln], 1)
            if ln == 1 and c == 0:
                v.memset(acc[0][:, :], 0.0).then_inc(acc0_zero, 1)

        def dve_ln_scale(v, b, ln, c):
            v.wait_ge(rstd_ready[ln], b * NG + c + 1)
            dst = chunk(z_sb if ln == 0 else x_res, c)
            v.tensor_tensor(dst, t_sb[c % 2], wide(rstd[:, c % 2, :]), ALU.mult).then_inc(ln_ready[ln], 1)

        def dve_ln2(v, b):
            for c in range(NG):
                if c >= 2:
                    dve_ln_scale(v, b, 1, c - 2)
                    v.wait_ge(ln_ready[1], b * NG + c - 1)
                dve_ln_center(v, b, 1, c)
            dve_ln_scale(v, b, 1, NG - 2)
            dve_ln_scale(v, b, 1, NG - 1)

        def dve_denominator(v, b):
            v.wait_ge(up_summed, b * (NB - G + 1) + NB - G + 1)
            v.tensor_scalar(denom[:, :], denom[:, :], 1.0, None, ALU.add).then_inc(den_step, 1)
            v.wait_ge(den_step, b * 2 + 1)
            v.reciprocal(denom[:, :], denom[:, :]).then_inc(den_step, 1)
            v.wait_ge(den_step, b * 2 + 2)

        def dve_w1(v, b3, b1):
            if b3 is None:
                v.memset(acc[0][:, :], 0.0).then_inc(acc0_zero, 1)
            if b1 is None:
                dve_denominator(v, b3)
                dve_ln2(v, b3)
                return
            for s in range(NS):
                if s == STRIP_NO[(2, 0, 0)] and b3 is not None:
                    dve_denominator(v, b3)
                    dve_ln2(v, b3)
                if s == STRIP_NO[(3, 0, 0)] and b3 is not None:
                    v.wait_ge(out_stored, b3 * 16 + 16)
                dve_s_strip(v, b1, s)
                if s > 0:
                    dve_k_strip(v, b1, s - 1)
                for j in range(NG - 1):
                    if s == DEGREES_AFTER[j]:
                        dve_degrees(v, b1, j)
            dve_k_strip(v, b1, NS - 1)
            dve_degrees(v, b1, NG - 1)
            dve_z(v, b1)

        def pool_setup(g):
            g.memset(ident[:, :], 1.0).then_inc(ident_made, 1)
            g.wait_ge(ident_made, 1)
            g.affine_select(ident[:, :], ident[:, :], pattern=[[1, P]], compare_op=ALU.is_equal, fill=0.0,
                            base=0, channel_multiplier=-1).then_inc(ident_made, 1)

        def pool_d(g, b):
            g.wait_ge(deg_step, b * 8 + 7)
            g.tensor_tensor(d_sb[:, :], deg[:, :], minus_half[:, :], ALU.pow).then_inc(d_ready, 1)

        def pool_rstd(g, b, ln):
            for c in range(NG):
                g.wait_ge(var_ready[ln], b * NG + c + 1)
                if c >= 2:
                    g.wait_ge(ln_ready[ln], b * NG + c - 1)
                g.tensor_tensor(rstd[:, c % 2, :], var[:, c % 2, :], minus_half[:, 0:G],
                                ALU.pow).then_inc(rstd_ready[ln], 1)

        def sp_w(sp, b, j):
            for n in range(j * G, (j + 1) * G):
                sp.dma_start(w_sb[:, n, 0:(j + 1) * SW], adj_v[b, :, n, 0:(j + 1) * SW]).then_inc(w_row[n], 16)
            for i in range(j):
                sp.dma_start(w_sb[:, i * G:(i + 1) * G, j * SW:(j + 1) * SW],
                             adj_v[b, :, i * G:(i + 1) * G, j * SW:(j + 1) * SW]).then_inc(w_col[(i, j)], 16)

        def sp_move(sp, b, j):
            sp.dma_start(u_move[j % 2], u_scratch[:, j * SW:(j + 1) * SW]).then_inc(move_in[j % 2], 16)

        def sp_w1(sp, b3, b1):
            if b3 is None:
                for j in range(2):
                    sp_w(sp, b1, j)
                sp.wait_ge(u_kept, 2 * NB)
                sp.dma_start(u_scratch[:, :], move_all).then_inc(u_stored, 16)
                sp.wait_ge(u_stored, 16)
                for j in range(2):
                    sp_move(sp, b1, j)
                sp_w(sp, b1, 2)
                for j in range(2, NG):
                    sp.wait_ge(v_ready, STRIP_NO[(j - 1, 0, 0)])
                    sp_move(sp, b1, j)
                sp_w(sp, b1, 3)
                sp.dma_start(z_sb[:, :, :], x_v[b1, :, :, :]).then_inc(z_in, 16)
                return
            if b1 is not None:
                for j in range(NG):
                    sp.wait_ge(freed, b3 * NG + j + 1)
                    sp_w(sp, b1, j)
                    if j >= 2:
                        sp.wait_ge(v_ready, b1 * NS + STRIP_NO[(j - 1, 0, 0)])
                        sp_move(sp, b1, j)
            sp.wait_ge(ln_ready[1], b3 * NG + NG)
            sp.dma_start(out_v[b3, :, :, :], x_res).then_inc(out_stored, 16)
            if b1 is not None:
                sp.dma_start(z_sb[:, :, :], x_v[b1, :, :, :]).then_inc(z_in, 16)

        def sp_p2(sp, b):
            sp.wait_ge(col_turned, b * COL_OUTS + COL_OUTS)
            for j in range(2):
                sp_move(sp, b, j)
            sp.wait_ge(scratch_free, b + 1)
            sp.dma_start(x_res, x_v[b, :, :, :]).then_inc(xres_in, 16)

        block = ctx.enter_context(nc.Block())

        @block.tensor
        def _(pe):
            pe_setup(pe)
            pe.wait_ge(const_made, 10)
            pe.wait_ge(ident_made, 2)
            pe_w1(pe, None, 0)
            pe_p2(pe, 0)
            with pe.Fori(0, B - 1, 1) as b:
                pe_w1(pe, b, b + 1)
                pe_p2(pe, b + 1)
            pe_w1(pe, B - 1, None)

        @block.scalar
        def _(act):
            act_setup(act)
            act_w1(act, None, 0)
            act_p2(act, 0)
            with act.Fori(0, B - 1, 1) as b:
                act_w1(act, b, b + 1)
                act_p2(act, b + 1)
            act_w1(act, B - 1, None)

        @block.vector
        def _(v):
            dve_setup(v)
            dve_w1(v, None, 0)
            dve_p2(v, 0)
            with v.Fori(0, B - 1, 1) as b:
                dve_w1(v, b, b + 1)
                dve_p2(v, b + 1)
            dve_w1(v, B - 1, None)

        @block.gpsimd
        def _(g):
            pool_setup(g)
            pool_d(g, 0)
            pool_rstd(g, 0, 0)
            with g.Fori(0, B - 1, 1) as b:
                pool_rstd(g, b, 1)
                pool_d(g, b + 1)
                pool_rstd(g, b + 1, 0)
            pool_rstd(g, B - 1, 1)

        @block.sync
        def _(sp):
            sp.dma_start(u_nat, u.rearrange("(n p) r -> p n r", p=P)).then_inc(small_in, 16)
            sp.dma_start(scale_sb[:, :], w_scale.to_broadcast([P, 1])).then_inc(small_in, 16)
            sp_w1(sp, None, 0)
            sp_p2(sp, 0)
            with sp.Fori(0, B - 1, 1) as b:
                sp_w1(sp, b, b + 1)
                sp_p2(sp, b + 1)
            sp_w1(sp, B - 1, None)
            sp.wait_ge(out_stored, 16 * B)
            for i in range(2):
                sp.wait_ge(move_in[i], 32 * B + 16)


def kernel(**inputs):
    import numpy as _np
    import concourse.bacc as _bacc
    from concourse import mybir as _mybir
    from concourse.bass_utils import run_bass_kernel_spmd as _run

    nc = _bacc.Bacc("TRN2", target_bir_lowering=False, num_devices=1)
    arrays, args = {}, []
    for name in ("x", "adj", "L0_gnn_U", "L0_gnn_w_scale"):
        a = _np.ascontiguousarray(inputs[name])
        if name == "L0_gnn_w_scale":
            a = a.reshape(1, 1)
        arrays[f"in_{name}"] = a
        args.append(nc.dram_tensor(f"in_{name}", a.shape, _mybir.dt.from_np(a.dtype), kind="ExternalInput").ap())
    args.append(nc.dram_tensor("out_x", (B, N, C), F32, kind="ExternalOutput").ap())
    args.append(nc.dram_tensor("u_scratch", (P, N), BF16, kind="Internal").ap())
    build(nc, *args)
    r = _run(nc, [arrays], core_ids=[0])
    return r.results[0]["out_x"]
```

```python
from contextlib import ExitStack

import concourse.bass as bass
from concourse import mybir

ALU = mybir.AluOpType
ACT = mybir.ActivationFunctionType
F32 = mybir.dt.float32
BF16 = mybir.dt.bfloat16
AX = mybir.AxisListType

P = 128
B, N, C = 8, 2048, 64
R = 16
NB = N // P
G = 4
NG = NB // G
SW = G * P
EPS_DEG = 1e-12
EPS_LN = 1e-5
TERMS = 8
H, M, L = 0, 1, 2
STAT_PARTS = (H, M, H, M, L, H, L, M)
MOVE_PARTS = (H, H, M, M, H, L, M, L)

STRIPS = [(j, i, r) for j in range(NG) for i in range(j + 1) for r in range(G)]
NS = len(STRIPS)
STRIP_NO = {s: n for n, s in enumerate(STRIPS)}
SUMS_AFTER = {}
for _j in range(NG):
    for _i in range(_j + 1):
        _s = STRIP_NO[(_j, _i, G - 1)] + 2
        if _j == 0:
            _s = STRIP_NO[(2, 0, 2)]
        if _j == 1:
            _s = STRIP_NO[(2, 0, 3)] + 2 * _i
        if _j == NG - 1 == _i:
            continue
        SUMS_AFTER.setdefault(_s, []).append((_i, _j))
SUM_ORDER = (2, 0, 1, 3)
COL_PARTS = [(_j, _h, G // 2) for _j in SUM_ORDER[:-1] for _h in (0, G // 2)] + [(NG - 1, 0, G)]
PART_AFTER = {STRIP_NO[(NG - 1, 0, 0)] + 1 + _n: _n for _n in range(len(COL_PARTS) - 1)}
KEEP_AFTER = {STRIP_NO[(NG - 1, 0, 0)] + 2 * _n + 4: _g for _n, _g in enumerate(SUM_ORDER[:-1])}
DEGREES_AT = {max([STRIP_NO[(NG - 1, _g, G - 1)] + 2] + [_s + 1 for _s in KEEP_AFTER if KEEP_AFTER[_s] == _g]): _g
              for _g in range(NG - 1)}
ROW_SUM_AFTER = {STRIP_NO[(1, 0, 1)] + _n: 2 * G + _n for _n in range(G)}
ROW_SUM_AFTER.update({STRIP_NO[(2, 0, 1)] + _n: 3 * G + _n for _n in range(G)})
LN2_START_AT = STRIP_NO[(2, 0, 0)]
LN2_MEAN_AFTER = STRIP_NO[(2, 1, 0)]
LN2_VAR_AFTER = STRIP_NO[(2, 2, 1)]
SUPERS = [(0, j) for j in (3, 0, 2, 1)] + [(i, j) for i in range(1, NG) for j in reversed(range(i, NG))]
ROW_END = [[s for s in SUPERS if s[0] == i][-1] for i in range(NG)]
EARLY = 2
EARLY_AFTER = {STRIP_NO[(NG - 1, 2, 1)] + _n: _n for _n in range(EARLY * G // 2)}
TURNS = [(i, j, r) for i, j in SUPERS for r in range(G) if not (i == j and r == G - 1)]
NT = len(TURNS)
P1_TURNS = [(i, j, r) for j in range(NG - 1) for i in range(j + 1) for r in range(G) if not (i == j and r == G - 1)]
P2_TURNS = [t for t in TURNS if t[1] == NG - 1]
P1_TURNS_FIRST = len([t for t in P1_TURNS if t[1] < NG - 2])
P1_TURN_AFTER = {STRIP_NO[(NG - 2, 0, 3)] + _n: _n for _n in range(P1_TURNS_FIRST)}
P1_TURN_AFTER.update({STRIP_NO[(NG - 1, 1, 1)] + _n: P1_TURNS_FIRST + _n
                      for _n in range(len(P1_TURNS) - P1_TURNS_FIRST)})
TURN_BANK = [1 if t[1] < NG - 2 else 2 for t in P1_TURNS]
LAST_UPPER_AFTER = STRIP_NO[(NG - 1, NG - 2, 0)]
UPPER = [(0, 1), (0, 2), (1, 2)]
UPPER_AFTER = {STRIP_NO[(1, 0, 1)]: [(0, 1)], STRIP_NO[(1, 1, 1)]: [(0, 2)], STRIP_NO[(1, 1, G - 1)]: [(1, 2)]}
UP_STEPS = len(UPPER) + (NG - 1) + 2
LAST_TURN = {(i, j): n for n, (i, j, r) in enumerate(TURNS)}

K_AT = {}
_at = 0
for _i, _j in SUPERS:
    for _r in range(G):
        K_AT[(_i, _j, _r)] = _at
        _at += SW if _i != _j else SW - P * _r
K_COLS = _at
LAST_STEPS = 11
LN2_STEPS = 8


def build(nc, x, adj, u, w_scale, out, u_scratch):
    with ExitStack() as ctx:
        def sb(name, shape, dt=F32):
            return ctx.enter_context(nc.sbuf_tensor(name, shape, dt))

        def sem(name):
            return ctx.enter_context(nc.semaphore(name))

        w_sb = sb("w_sb", [P, NB, N])
        k_sb = sb("k_sb", [P, K_COLS])
        z_sb = sb("z_sb", [P, NB, C])
        u_stat = sb("u_stat", [P, N], BF16)
        colsum_sb = sb("colsum_sb", [P, SW])
        u_move = [colsum_sb[:, i * SW // 2:(i + 1) * SW // 2].bitcast(BF16) for i in range(2)]
        ident = sb("ident", [P, P])
        ones = sb("ones", [P, 32])
        pick = sb("pick", [P, 1])
        row_parts = sb("row_parts", [P, NB, NG])
        deg = sb("deg", [P, NB])
        d_sb = sb("d_sb", [P, NB])
        scaled_d = sb("scaled_d", [P, NB])
        w_low = sb("w_low", [P, NB])
        w_up = sb("w_up", [P, NG - 1, NB])
        denom = sb("denom", [P, NB])
        scale_sb = sb("scale_sb", [P, 1])
        minus_half = sb("minus_half", [P, NB])
        mean = sb("mean", [P, 2, G])
        var = sb("var", [P, 2, G])
        rstd = sb("rstd", [P, 2, G])
        mean2 = deg
        var2 = rstd2 = scaled_d

        acc_all = ctx.enter_context(nc.psum_tensor("acc", [P, NG, SW], F32))
        acc = [acc_all[:, c, :] for c in range(NG)]
        col_acc = [acc[c] for c in (0, 3, 2, 1)]
        ps_w = [ctx.enter_context(nc.psum_tensor(f"ps_w{i}", [P, SW], F32)) for i in range(2)]
        ps_a = [ctx.enter_context(nc.psum_tensor(f"ps_a{i}", [P, SW], F32)) for i in range(2)]

        x_res = k_sb[:, 0:NB * C].rearrange("p (n c) -> p n c", c=C)
        y_res = k_sb[:, NB * C:NB * C + SW]
        t_sb = [k_sb[:, NB * C + SW + i * G * C:NB * C + SW + (i + 1) * G * C].rearrange("p (n c) -> p n c", c=C)
                for i in range(2)]
        at23, at33 = K_AT[(NG - 2, NG - 1, 0)], K_AT[(NG - 1, NG - 1, 0)]
        y_four = [k_sb[:, at23 + i * SW:at23 + (i + 1) * SW] for i in range(NG)]
        sq2 = k_sb[:, at23:at23 + NB * C].rearrange("p (n c) -> p n c", c=C)
        res2 = k_sb[:, at33:at33 + NB * C].rearrange("p (n c) -> p n c", c=C)

        def in_w(row, cols, dt=F32):
            ap = w_sb[:, row, 0:cols]
            return ap if dt == F32 else ap.bitcast(dt)

        u_nat = in_w(12, NB * R).rearrange("p (n r) -> p n r", r=R)
        u_rest = w_sb[:, 12, 512:512 + NB * R].rearrange("p (n r) -> p n r", r=R)
        u_part = [w_sb[:, 12, 1024 + 128 * i:1024 + 128 * (i + 1)].bitcast(BF16).rearrange("p (n r) -> p n r", r=R)
                  for i in range(3)]
        ident_b = w_sb[:, 12, 1536:1600].bitcast(BF16)
        cat_stat = in_w(13, NB * P // 2, BF16).rearrange("p (n g r) -> p n g r", g=TERMS, r=R)
        cat_move = in_w(14, NB * P // 2, BF16).rearrange("p (n g r) -> p n g r", g=TERMS, r=R)
        move_all = in_w(15, N // 2, BF16)

        small_in = sem("small_in")
        ident_made = sem("ident_made")
        const_made = sem("const_made")
        u_split = sem("u_split")
        u_turned = sem("u_turned")
        u_kept = sem("u_kept")
        u_stored = sem("u_stored")
        w_row = [sem(f"w_row{n}") for n in range(NB)]
        w_col = {(i, j): sem(f"w_col{i}{j}") for j in range(NG) for i in range(j)}
        move_in = [sem(f"move_in{i}") for i in range(2)]
        z_in = sem("z_in")
        xres_in = sem("xres_in")
        out_stored = sem("out_stored")
        low_summed = sem("low_summed")
        v_ready = sem("v_ready")
        gate_ready = sem("gate_ready")
        wt_ready = sem("wt_ready")
        s_ready = sem("s_ready")
        wt_kept = sem("wt_kept")
        k_ready = sem("k_ready")
        acc0_zero = sem("acc0_zero")
        col_ready = sem("col_ready")
        col_out = sem("col_out")
        col_turned = sem("col_turned")
        sums_kept = sem("sums_kept")
        deg_step = sem("deg_step")
        d_ready = sem("d_ready")
        z_ready = sem("z_ready")
        scaled_ready = sem("scaled_ready")
        used_straight = sem("used_straight")
        kt_ready = sem("kt_ready")
        kt_kept = sem("kt_kept")
        up_summed = sem("up_summed")
        wu_ready = sem("wu_ready")
        wu_kept = sem("wu_kept")
        wu1_ready = sem("wu1_ready")
        wu1_kept = sem("wu1_kept")
        scratch_free = sem("scratch_free")
        y_ready = sem("y_ready")
        y_out = [sem(f"y_out{i}") for i in (1, 2)]
        yn_ready = [sem(f"yn_ready{i}") for i in (1, 2)]
        ln_step = [sem(f"ln_step{i}") for i in (1, 2)]
        var_ready = [sem(f"var_ready{i}") for i in (1, 2)]
        rstd_ready = [sem(f"rstd_ready{i}") for i in (1, 2)]
        ln_ready = [sem(f"ln_ready{i}") for i in (1, 2)]
        den_step = sem("den_step")
        last_step = sem("last_step")
        ln_pool = sem("ln_pool")
        rows_freed = sem("rows_freed")
        freed = sem("freed")
        chunk_done = sem("chunk_done")

        adj_v = adj.rearrange("b (n p) m -> b p n m", p=P)
        x_v = x.rearrange("b (n p) c -> b p n c", p=P)
        out_v = out.rearrange("b (n p) c -> b p n c", p=P)

        def first_col(i, j, r):
            return i * G + r if i == j else j * G

        def k_strip(i, j, r):
            w = (SW - P * r) if i == j else SW
            at = K_AT[(i, j, r)]
            return k_sb[:, at:at + w]

        def turned_cols(i, j, r):
            return (i * G + r + 1, G - 1 - r) if i == j else (j * G, G)

        def k_turned(i, j, r):
            w = turned_cols(i, j, r)[1] * P
            at = K_AT[(i, j, r)] + (P if i == j else 0)
            return k_sb[:, at:at + w]

        def pe_setup(pe):
            pe.wait_ge(u_split, 6 + 2 * TERMS)
            for n in range(2 * NG):
                if n >= 2:
                    pe.wait_ge(u_kept, n - 1)
                for q in range(G):
                    cat = (cat_move if n < NG else cat_stat)[:, n % NG * G + q, :, :].rearrange("p g r -> p (g r)")
                    m = pe.matmul(ps_w[n % 2][:, q * P:(q + 1) * P], cat, ident_b, start=True, stop=True)
                m.then_inc(u_turned, 1)
            pe.wait_ge(u_kept, 2 * NG)

        def pe_p1_strip(pe, b, s):
            j, i, r = STRIPS[s]
            row = i * G + r
            c0 = first_col(i, j, r)
            blocks = (j + 1) * G - c0
            if (i, r) == (0, 0):
                pe.wait_ge(low_summed, b * NB + (j + 1) * G)
            if s >= 2:
                pe.wait_ge(wt_kept, b * NS + s - 1)
            for q in range(blocks):
                t = pe.transpose(ps_w[s % 2][:, q * P:(q + 1) * P],
                                 w_sb[:, c0 + q, row * P:(row + 1) * P], ident[:, :])
            t.then_inc(wt_ready, 1)
            if (i, r) == (0, 0):
                pe.wait_ge(move_in[j % 2], b * 32 + 16 * (j // 2 + 1))
            if s >= 2:
                pe.wait_ge(k_ready, b * NS + s - 1)
            off = (c0 - j * G) * P
            pe.matmul(ps_a[s % 2][:, 0:blocks * P], u_stat[:, row * P:(row + 1) * P], u_move[j % 2][:, off:SW],
                      start=True, stop=True).then_inc(v_ready, 1)

        def pe_colsum(pe, b3, b, i, j):
            rows = G if i < j else G - 1
            pe.wait_ge(k_ready, b * NS + STRIP_NO[(j, i, rows - 1)] + 1)
            if i == 0:
                if j == 0:
                    pe.wait_ge(acc0_zero, b + 1)
                elif b3 is not None:
                    pe.wait_ge(ln_step[1], b3 * LN2_STEPS + 2)
            for r in range(rows):
                rhs = k_strip(i, j, r) if i < j else k_turned(i, j, r)
                c = 0 if i < j else (r + 1) * P
                m = pe.matmul(col_acc[j][32 * r:32 * r + 32, c:SW], ones[:, :], rhs,
                              start=(i == 0 and j > 0), stop=True, skip_group_check=True,
                              tile_position=(0, 32 * r))
            if i == j:
                m.then_inc(col_ready, 1)

        def pe_colturn(pe, b, n):
            j, first, blocks = COL_PARTS[n]
            pe.wait_ge(col_out, b * len(COL_PARTS) + n + 1)
            for q in range(blocks):
                m = pe.matmul(col_acc[j][:, first + q:first + q + 1], colsum_sb[:, q * P:(q + 1) * P], pick[:, :],
                              start=True, stop=True)
            m.then_inc(col_turned, 1)

        def straight(i, j):
            return [(j, r % 2, i * G + r, k_strip(i, j, r), (P * r if i == j else 0)) for r in range(G)]

        def turned(i, j):
            if i != j:
                at = K_AT[(i, j, 0)]
                quad = k_sb[:, at:at + G * SW].rearrange("p (r m) -> p r m", r=G)
                return [(i, q % 2, j * G + q, quad[:, :, q * P:(q + 1) * P], 0) for q in range(G)]
            found = []
            for r in range(G - 1):
                for q in range(r + 1, G):
                    at = K_AT[(i, i, r)] + (q - r) * P
                    found.append((i, q % 2, i * G + q, k_sb[:, at:at + P], r * P))
            return found

        def pe_products(pe, products, begun):
            for c, half, m, rhs, at in products:
                width = rhs.shape[-1] * (rhs.shape[1] if len(rhs.shape) == 3 else 1)
                mm = pe.matmul(acc[c][64 * half:64 * half + 64, at:at + width], z_sb[:, m, :], rhs,
                               start=(c, half) not in begun, stop=True, skip_group_check=True,
                               tile_position=(0, 64 * half))
                begun.add((c, half))
            return mm

        def pe_turn(pe, b, t):
            i, j, r = TURNS[t]
            c0, blocks = turned_cols(i, j, r)
            if t >= 2:
                pe.wait_ge(kt_kept, b * NT + t - 1)
            for q in range(blocks):
                m = pe.transpose(ps_a[t % 2][:, q * P:(q + 1) * P], k_turned(i, j, r)[:, q * P:(q + 1) * P], ident[:, :])
            m.then_inc(kt_ready, 1)
            if (i, j, r) in P2_TURNS:
                n = P2_TURNS.index((i, j, r))
                if n >= 2:
                    pe.wait_ge(wu_kept, b * len(P2_TURNS) + n - 1)
                for q in range(blocks):
                    m = pe.transpose(ps_w[n % 2][:, q * P:(q + 1) * P],
                                     w_sb[:, i * G + r, (c0 + q) * P:(c0 + q + 1) * P], ident[:, :])
                m.then_inc(wu_ready, 1)

        def pe_p1_turn(pe, b3, b, n):
            i, j, r = P1_TURNS[n]
            c0, blocks = turned_cols(i, j, r)
            if n == 0 and b3 is not None:
                pe.wait_ge(ln_step[1], b3 * LN2_STEPS + 2)
            if n == P1_TURNS_FIRST:
                pe.wait_ge(sums_kept, b * NG + 1)
            if n > 0:
                pe.wait_ge(wu1_kept, b * len(P1_TURNS) + n)
            for q in range(blocks):
                m = pe.transpose(acc[TURN_BANK[n]][:, q * P:(q + 1) * P],
                                 w_sb[:, i * G + r, (c0 + q) * P:(c0 + q + 1) * P], ident[:, :])
            m.then_inc(wu1_ready, 1)

        def pe_yn(pe, b, ln, c):
            pe.wait_ge(y_out[ln], b * NG + c + 1)
            for q in range(G):
                m = pe.transpose(acc[c][:, q * P:(q + 1) * P], (y_four[c] if ln else y_res)[:, q * P:(q + 1) * P],
                                 ident[:, :])
            m.then_inc(yn_ready[ln], 1)

        def pe_early(pe, b, n, begun):
            if n == 0:
                pe.wait_ge(z_ready, b * NG + 1)
                pe.wait_ge(sums_kept, b * NG + 3)
            i, j = SUPERS[n * 2 // G]
            r = n * 2 % G
            m = pe_products(pe, straight(i, j)[r:r + 2], begun)
            if r + 2 == G:
                m.then_inc(used_straight, 1)

        def pe_finish(pe, b, s, begun):
            i, j = SUPERS[s]
            pe.wait_ge(kt_kept, b * NT + LAST_TURN[(i, j)] + 1)
            m = pe_products(pe, turned(i, j), begun)
            if s == 0:
                m.then_inc(scratch_free, 1)
            if (i, j) == ROW_END[i]:
                m.then_inc(y_ready, 1)

        def pe_p2_end(pe, b):
            pe_finish(pe, b, len(SUPERS) - 1, {(NG - 1, 0), (NG - 1, 1)})
            pe_yn(pe, b, 0, NG - 1)

        def pe_p2(pe, b, begun):
            pe.wait_ge(wt_kept, b * NS + NS)
            pe.wait_ge(k_ready, b * NS + NS)

            for s, (i, j) in enumerate(SUPERS):
                if s >= EARLY:
                    pe_products(pe, straight(i, j), begun).then_inc(used_straight, 1)
                turns = [t for t in range(NT) if TURNS[t][:2] == (i, j)]
                for t in turns[:2]:
                    pe_turn(pe, b, t)
                    if t == 0:
                        pe_colturn(pe, b, len(COL_PARTS) - 1)
                if s == 1:
                    pe.wait_ge(z_ready, b * NG + NG)
                if s > 0:
                    pe_finish(pe, b, s - 1, begun)
                for t in turns[2:]:
                    pe_turn(pe, b, t)
                if s > 0 and SUPERS[s - 1] == ROW_END[i - 1]:
                    pe_yn(pe, b, 0, i - 1)
        def p3_products(k):
            pairs = [(m, k) for m in range((k + 1) * G)]
            pairs += [(m, c) for c in range(k) for m in range(k * G, (k + 1) * G)]
            return [(c, m % 2, m, w_sb[:, c * G:(c + 1) * G, m * P:(m + 1) * P], 0) for m, c in pairs]

        def pe_last_p3(pe, b):
            pe.wait_ge(wu1_kept, (b + 1) * len(P1_TURNS))
            for c in range(NG):
                begun = set()
                for k in range(NG):
                    if c == 0:
                        pe.wait_ge(ln_ready[0], b * NG + k + 1)
                    if (c, k) == (0, 1):
                        pe_p2_end(pe, b)
                    if (c, k) == (0, NG - 1):
                        pe.wait_ge(wu_kept, (b + 1) * len(P2_TURNS))
                    m = pe_products(pe, [(c, m % 2, m, w_sb[:, c * G:(c + 1) * G, m * P:(m + 1) * P], 0)
                                         for m in range(k * G, (k + 1) * G)], begun)
                m.then_inc(chunk_done, 1)
                if c > 0:
                    pe_yn(pe, b, 1, c - 1)
            pe_yn(pe, b, 1, NG - 1)

        def pe_w1(pe, b3, b1, p2_begun):
            begun = set()
            strips = list(range(NS)) if b1 is not None else []
            by_j = [[s for s in strips if STRIPS[s][0] == j] for j in range(NG)]
            if b1 is None:
                pe_last_p3(pe, b3)
                return
            if b3 is not None:
                pe.wait_ge(wu1_kept, (b3 + 1) * len(P1_TURNS))
                for k in range(NG):
                    pe.wait_ge(ln_ready[0], b3 * NG + k + 1)
                    if k == NG - 1:
                        pe.wait_ge(wu_kept, (b3 + 1) * len(P2_TURNS))
                    products = p3_products(k)
                    rows_end = (k + 1) * G
                    among = by_j[k - 2] if k >= 2 else []
                    share = -(-len(products) // (len(among) + 1))
                    for n in range(len(among) + 1):
                        for first, end in ((n * share, min((n + 1) * share, rows_end)),
                                           (max(n * share, rows_end), (n + 1) * share)):
                            if products[first:end]:
                                m = pe_products(pe, products[first:end], begun)
                                if end == rows_end:
                                    m.then_inc(rows_freed, 1)
                                if k > 0 and end >= len(products):
                                    m.then_inc(freed, 1)
                        if n < len(among):
                            pe_p1_strip(pe, b1, among[n])
                    if k == 0:
                        pe_p2_end(pe, b3)
            if b1 is not None:
                for s in range(0 if b3 is None else STRIP_NO[(2, 0, 0)], NS):
                    pe_p1_strip(pe, b1, s)
                    if s == LN2_START_AT and b3 is not None:
                        for c in range(NG):
                            pe_yn(pe, b3, 1, c)
                    if s >= STRIP_NO[(2, 0, 2)]:
                        for i, j in SUMS_AFTER.get(s, ()):
                            pe_colsum(pe, b3, b1, i, j)
                    if s - 1 in PART_AFTER:
                        pe_colturn(pe, b1, PART_AFTER[s - 1])
                    if s in P1_TURN_AFTER:
                        pe_p1_turn(pe, b3, b1, P1_TURN_AFTER[s])
                    if s in EARLY_AFTER:
                        pe_early(pe, b1, EARLY_AFTER[s], p2_begun)
                pe_colsum(pe, b3, b1, NG - 1, NG - 1)

        def act_setup(act):
            for n in range(2 * NG):
                act.wait_ge(u_turned, n + 1)
                dst = (move_all if n < NG else u_stat)[:, n % NG * SW:(n % NG + 1) * SW]
                act.activation(dst, ps_w[n % 2][:, :], ACT.Copy).then_inc(u_kept, 1)

        def act_row_sum(act, b, n):
            act.wait_ge(w_row[n], b * 16 + 16)
            row = w_sb[:, n, 0:(n // G + 1) * SW]
            act.activation(row, row, ACT.Copy, accum_out=w_low[:, n:n + 1]).then_inc(low_summed, 1)

        def act_gate(act, b, s):
            j, i, r = STRIPS[s]
            w = ((j + 1) * G - first_col(i, j, r)) * P
            act.wait_ge(v_ready, b * NS + s + 1)
            act.activation(ps_a[s % 2][:, 0:w], ps_a[s % 2][:, 0:w], ACT.Sigmoid).then_inc(gate_ready, 1)

        def act_keep_wt(act, b, s):
            j, i, r = STRIPS[s]
            c0, row = first_col(i, j, r), i * G + r
            blocks = (j + 1) * G - c0
            act.wait_ge(s_ready, b * NS + s + 1)
            act.activation(w_sb[:, c0:c0 + blocks, row * P:(row + 1) * P],
                           ps_w[s % 2][:, 0:blocks * P].rearrange("p (q m) -> p q m", q=blocks),
                           ACT.Copy).then_inc(wt_kept, 1)

        def act_p1_turn(act, b, n):
            i, j, r = P1_TURNS[n]
            c0, blocks = turned_cols(i, j, r)
            if i < j and r == 0:
                act.wait_ge(up_summed, b * UP_STEPS + UPPER.index((i, j)) + 1)
            act.wait_ge(wu1_ready, b * len(P1_TURNS) + n + 1)
            act.activation(w_sb[:, i * G + r, c0 * P:(c0 + blocks) * P], acc[TURN_BANK[n]][:, 0:blocks * P],
                           ACT.Copy).then_inc(wu1_kept, 1)

        def act_p1(act, b3, b):
            for s in range(NS):
                j, i, r = STRIPS[s]
                if s > 0:
                    act_keep_wt(act, b, s - 1)
                if s - 1 in P1_TURN_AFTER:
                    act_p1_turn(act, b, P1_TURN_AFTER[s - 1])
                if (i, r) == (0, 0) and j < 2:
                    for n in range(j * G, (j + 1) * G):
                        act_row_sum(act, b, n)
                if b3 is not None and s == LN2_START_AT:
                    for c in range(NG):
                        act_y_out(act, b3, 1, c)
                act_gate(act, b, s)
                if s in PART_AFTER:
                    act_col_out(act, b, PART_AFTER[s])
                if s in ROW_SUM_AFTER:
                    act_row_sum(act, b, ROW_SUM_AFTER[s])
            act_keep_wt(act, b, NS - 1)
            if NS - 1 in P1_TURN_AFTER:
                act_p1_turn(act, b, P1_TURN_AFTER[NS - 1])
            act_col_out(act, b, len(COL_PARTS) - 1)

        def act_col_out(act, b, n):
            j, first, blocks = COL_PARTS[n]
            if first == 0:
                act.wait_ge(col_ready, b * NG + j + 1)
            if n > 0:
                act.wait_ge(col_turned, b * len(COL_PARTS) + n)
            act.activation(colsum_sb[:, 0:blocks * P], col_acc[j][:, first * P:(first + blocks) * P], ACT.Copy)\
             .then_inc(col_out, 1)

        def act_y_out(act, b, ln, c, last=False):
            if ln == 0:
                act.wait_ge(y_ready, b * NG + c + 1)
            else:
                if last:
                    act.wait_ge(chunk_done, c + 1)
                else:
                    act.wait_ge(freed, (b + 1) * (NG - 1))
            if ln == 0 and c > 0:
                act.wait_ge(yn_ready[ln], b * NG + c)
            act.activation((y_four[c] if ln else y_res), acc[c], ACT.Copy).then_inc(y_out[ln], 1)

        def act_p2(act, b):
            for t, (i, j, r) in enumerate(TURNS):
                act.wait_ge(used_straight, b * len(SUPERS) + SUPERS.index((i, j)) + 1)
                act.wait_ge(kt_ready, b * NT + t + 1)
                w = turned_cols(i, j, r)[1] * P
                act.activation(k_turned(i, j, r), ps_a[t % 2][:, 0:w], ACT.Copy).then_inc(kt_kept, 1)
                if i > 0 and j == NG - 1 and r == 1:
                    if i == 1:
                        act.wait_ge(scratch_free, b + 1)
                    act_y_out(act, b, 0, i - 1)
            act_y_out(act, b, 0, NG - 1)

        def act_w1(act, b3, b1):
            if b1 is not None:
                act_p1(act, b3, b1)
            else:
                for c in range(NG):
                    act_y_out(act, b3, 1, c, last=True)

        def dve_setup(v):
            v.memset(ones[:, :], 1.0).then_inc(const_made, 1)
            v.memset(pick[:, :], 0.0).then_inc(const_made, 1)
            v.memset(row_parts[:, :, :], 0.0).then_inc(const_made, 1)
            v.memset(w_up[:, :, :], 0.0).then_inc(const_made, 1)
            v.memset(minus_half[:, :], -0.5).then_inc(const_made, 1)
            v.wait_ge(const_made, 2)
            for g in range(4):
                v.memset(pick[32 * g:32 * g + 1, :], 1.0).then_inc(const_made, 1)
            v.wait_ge(ident_made, 2)
            v.wait_ge(small_in, 32)
            v.tensor_copy(ident_b, ident[:, :]).then_inc(u_split, 1)
            v.tensor_copy(u_part[H], u_nat).then_inc(u_split, 1)
            v.wait_ge(u_split, 2)
            v.tensor_tensor(u_rest, u_nat, u_part[H], ALU.subtract).then_inc(u_split, 1)
            v.wait_ge(u_split, 3)
            v.tensor_copy(u_part[M], u_rest).then_inc(u_split, 1)
            v.wait_ge(u_split, 4)
            v.tensor_tensor(u_nat, u_rest, u_part[M], ALU.subtract).then_inc(u_split, 1)
            v.wait_ge(u_split, 5)
            v.tensor_copy(u_part[L], u_nat).then_inc(u_split, 1)
            v.wait_ge(u_split, 6)
            for g in range(TERMS):
                v.tensor_copy(cat_stat[:, :, g, :], u_part[STAT_PARTS[g]]).then_inc(u_split, 1)
                v.tensor_copy(cat_move[:, :, g, :], u_part[MOVE_PARTS[g]]).then_inc(u_split, 1)

        def dve_s_strip(v, b, s):
            j, i, r = STRIPS[s]
            c0, row = first_col(i, j, r), i * G + r
            blocks = (j + 1) * G - c0
            if i < j and r == 0:
                v.wait_ge(w_col[(i, j)], b * 16 + 16)
            v.wait_ge(wt_ready, b * NS + s + 1)
            v.tensor_tensor(k_strip(i, j, r), w_sb[:, row, c0 * P:(c0 + blocks) * P], ps_w[s % 2][:, 0:blocks * P],
                            ALU.add).then_inc(s_ready, 1)

        def dve_k_strip(v, b, s):
            j, i, r = STRIPS[s]
            dst = k_strip(i, j, r)
            v.wait_ge(s_ready, b * NS + s + 1)
            v.wait_ge(gate_ready, b * NS + s + 1)
            v.scalar_tensor_tensor(out=dst, in0=dst, scalar=0.5, in1=ps_a[s % 2][:, 0:dst.shape[-1]],
                                   op0=ALU.mult, op1=ALU.mult,
                                   accum_out=row_parts[:, i * G + r, j:j + 1]).then_inc(k_ready, 1)

        def of_group(ap, g):
            return ap[:, g * G:(g + 1) * G]

        def dve_keep_sums(v, b, g):
            v.wait_ge(col_turned, b * len(COL_PARTS) + min(2 * SUM_ORDER.index(g) + 2, len(COL_PARTS)))
            v.tensor_copy(of_group(deg, g), col_acc[g][:, 0:G]).then_inc(sums_kept, 1)

        def dve_degrees(v, b, g, step):
            done = (b * NG + g) * 3
            if step == 0:
                v.wait_ge(k_ready, b * NS + STRIP_NO[(NG - 1, g, G - 1)] + 1)
                v.tensor_reduce(of_group(d_sb, g), row_parts[:, g * G:(g + 1) * G, :], AX.X, ALU.add).then_inc(deg_step, 1)
            if step == 1:
                v.wait_ge(sums_kept, b * NG + SUM_ORDER.index(g) + 1)
                v.wait_ge(deg_step, done + 1)
                v.tensor_tensor(of_group(deg, g), of_group(deg, g), of_group(d_sb, g), ALU.add).then_inc(deg_step, 1)
            if step == 2:
                v.wait_ge(deg_step, done + 2)
                v.tensor_scalar(of_group(deg, g), of_group(deg, g), EPS_DEG, None, ALU.max).then_inc(deg_step, 1)

        def dve_upper_sums(v, b, i, j):
            if j < NG - 1:
                v.wait_ge(w_col[(i, j)], b * 16 + 16)
            v.tensor_reduce(w_up[:, j - 1, i * G:(i + 1) * G], w_sb[:, i * G:(i + 1) * G, j * SW:(j + 1) * SW],
                            AX.X, ALU.add).then_inc(up_summed, 1)

        def dve_p2(v, b):
            for t, (i, j, r) in enumerate(TURNS):
                c0, blocks = turned_cols(i, j, r)
                row = i * G + r
                if j == NG - 1 and i < NG - 1 and r == 0:
                    if i > 0:
                        dve_upper_sums(v, b, i, j)
                    v.wait_ge(up_summed, b * UP_STEPS + len(UPPER) + i + 1)
                if j == NG - 1:
                    n = P2_TURNS.index((i, j, r))
                    v.wait_ge(wu_ready, b * len(P2_TURNS) + n + 1)
                    v.tensor_copy(w_sb[:, row, c0 * P:(c0 + blocks) * P],
                                  ps_w[n % 2][:, 0:blocks * P]).then_inc(wu_kept, 1)
                if t == LAST_TURN[(0, NG - 1)]:
                    v.wait_ge(d_ready, (b + 1) * NG)
                    v.tensor_scalar(scaled_d[:, :], d_sb[:, :], scale_sb[:, 0:1], None, ALU.mult).then_inc(scaled_ready, 1)
                if t == LAST_TURN[(NG - 2, NG - 1)]:
                    v.tensor_reduce(denom[:, :], w_up.rearrange("p j n -> p n j"), AX.X, ALU.add).then_inc(up_summed, 1)
                if t == LAST_TURN[(NG - 2, NG - 2)]:
                    v.wait_ge(up_summed, (b + 1) * UP_STEPS - 1)
                    v.tensor_tensor(denom[:, :], denom[:, :], w_low[:, :], ALU.add).then_inc(up_summed, 1)
                if t == LAST_TURN[(NG - 1, NG - 1)]:
                    dve_denominator(v, b)
                if i > 0 and t == LAST_TURN[(i, NG - 1)]:
                    dve_ln1_center(v, b, i - 1)
                if 0 < i < NG - 1 and t == LAST_TURN[(i, NG - 1)] + 2:
                    dve_ln1_scale(v, b, i - 1)
            dve_ln1_scale(v, b, NG - 2)
            dve_ln1_center(v, b, NG - 1)
            dve_ln1_scale(v, b, NG - 1)

        def chunk(ap, c):
            return ap[:, c * G:(c + 1) * G, :]

        def spread(ap, n):
            return ap.unsqueeze(2).to_broadcast([P, n, C])

        def dve_variance(v, t, sq, mu, var_out, step, done, ready):
            n = t.shape[1]
            v.wait_ge(step, done)
            v.tensor_reduce(mu, t, AX.X, ALU.add).then_inc(step, 1)
            v.wait_ge(step, done + 1)
            v.tensor_scalar(mu, mu, 1.0 / C, None, ALU.mult).then_inc(step, 1)
            v.wait_ge(step, done + 2)
            v.tensor_tensor(t, t, spread(mu, n), ALU.subtract).then_inc(step, 1)
            v.wait_ge(step, done + 3)
            v.tensor_tensor(sq, t, t, ALU.mult).then_inc(step, 1)
            v.wait_ge(step, done + 4)
            v.tensor_reduce(var_out, sq, AX.X, ALU.add).then_inc(step, 1)
            v.wait_ge(step, done + 5)
            v.tensor_scalar(var_out, var_out, 1.0 / C, EPS_LN, ALU.mult, ALU.add).then_inc(ready, 1)

        def dve_ln1_center(v, b, c):
            t = t_sb[c % 2]
            yn = acc[c].rearrange("p (n h c) -> p n h c", h=2, c=C)
            sq = yn[:, :, 0, :]
            done = (b * NG + c) * 9
            v.wait_ge(yn_ready[0], b * NG + c + 1)
            v.wait_ge(scaled_ready, b + 1)
            v.tensor_copy(t, yn[:, :, 0, :]).then_inc(ln_step[0], 1)
            v.wait_ge(ln_step[0], done + 1)
            v.tensor_tensor(t, t, yn[:, :, 1, :], ALU.add).then_inc(ln_step[0], 1)
            v.wait_ge(ln_step[0], done + 2)
            v.tensor_tensor(t, t, spread(of_group(scaled_d, c), G), ALU.mult).then_inc(ln_step[0], 1)
            v.wait_ge(xres_in, b * 16 + 16)
            v.wait_ge(ln_step[0], done + 3)
            v.tensor_tensor(t, t, chunk(x_res, c), ALU.add).then_inc(ln_step[0], 1)
            dve_variance(v, t, sq, mean[:, c % 2, :], var[:, c % 2, :], ln_step[0], done + 4, var_ready[0])

        def dve_ln1_scale(v, b, c):
            v.wait_ge(rstd_ready[0], b * NG + c + 1)
            v.tensor_tensor(chunk(z_sb, c), t_sb[c % 2], spread(rstd[:, c % 2, :], G), ALU.mult).then_inc(ln_ready[0], 1)

        def dve_ln2_start(v, b):
            step, done = ln_step[1], b * LN2_STEPS
            yn = acc_all[:, :, :].rearrange("p g (n h c) -> p (g n) h c", h=2, c=C)
            v.wait_ge(yn_ready[1], b * NG + NG)
            v.tensor_tensor(res2, yn[:, :, 0, :], z_sb[:, :, :], ALU.add).then_inc(step, 1)
            v.wait_ge(step, done + 1)
            v.tensor_tensor(res2, res2, yn[:, :, 1, :], ALU.add).then_inc(step, 1)

        def dve_ln2_scale(v, b):
            step, done = ln_step[1], b * LN2_STEPS
            v.wait_ge(step, done + 2)
            v.memset(acc[0], 0.0).then_inc(acc0_zero, 1)
            v.tensor_tensor(res2, res2, spread(denom[:, :], NB), ALU.mult).then_inc(step, 1)

        def dve_ln2_no_nan(v, b):
            step, done = ln_step[1], b * LN2_STEPS
            v.wait_ge(step, done + 3)
            v.tensor_scalar(sq2, res2, 0.0, None, ALU.max).then_inc(step, 1)
            v.wait_ge(step, done + 4)
            v.scalar_tensor_tensor(out=res2, in0=res2, scalar=0.0, in1=sq2, op0=ALU.min, op1=ALU.add).then_inc(step, 1)

        def dve_ln2_mean(v, b):
            v.wait_ge(ln_pool, b * 3 + 1)
            v.tensor_reduce(mean2[:, :], res2, AX.X, ALU.add).then_inc(ln_step[1], 1)
            v.wait_ge(ln_step[1], b * LN2_STEPS + 6)
            v.tensor_scalar(mean2[:, :], mean2[:, :], 1.0 / C, None, ALU.mult).then_inc(ln_step[1], 1)

        def dve_ln2_var(v, b):
            v.wait_ge(ln_pool, b * 3 + 3)
            v.tensor_reduce(var2[:, :], sq2, AX.X, ALU.add).then_inc(ln_step[1], 1)
            v.wait_ge(ln_step[1], b * LN2_STEPS + 8)
            v.tensor_scalar(var2[:, :], var2[:, :], 1.0 / C, EPS_LN, ALU.mult, ALU.add).then_inc(var_ready[1], 1)

        def dve_last_ln2(v, b, c):
            t, sq, x1 = chunk(res2, c), chunk(sq2, c), chunk(z_sb, c)
            yn = acc[c].rearrange("p (n h c) -> p n h c", h=2, c=C)
            rows = slice(c * G, (c + 1) * G)
            done = c * LAST_STEPS
            v.wait_ge(yn_ready[1], b * NG + c + 1)
            v.tensor_tensor(t, yn[:, :, 0, :], x1, ALU.add).then_inc(last_step, 1)
            v.wait_ge(last_step, done + 1)
            v.tensor_tensor(t, t, yn[:, :, 1, :], ALU.add).then_inc(last_step, 1)
            v.wait_ge(last_step, done + 2)
            v.tensor_tensor(t, t, spread(denom[:, rows], G), ALU.mult).then_inc(last_step, 1)
            v.wait_ge(last_step, done + 3)
            v.tensor_scalar(sq, t, 0.0, None, ALU.max).then_inc(last_step, 1)
            v.wait_ge(last_step, done + 4)
            v.scalar_tensor_tensor(out=t, in0=t, scalar=0.0, in1=sq, op0=ALU.min, op1=ALU.add).then_inc(last_step, 1)
            v.wait_ge(last_step, done + 5)
            v.tensor_tensor(t, t, x1, ALU.add).then_inc(last_step, 1)
            dve_variance(v, t, sq, mean2[:, rows], var2[:, rows], last_step, done + 6, var_ready[1])
            v.wait_ge(rstd_ready[1], b + c + 1)
            v.tensor_tensor(t, t, spread(rstd2[:, rows], G), ALU.mult).then_inc(ln_ready[1], 1)

        def dve_denominator(v, b):
            v.wait_ge(up_summed, (b + 1) * UP_STEPS)
            v.tensor_scalar(denom[:, :], denom[:, :], 1.0, None, ALU.add).then_inc(den_step, 1)
            v.wait_ge(den_step, b * 2 + 1)
            v.reciprocal(denom[:, :], denom[:, :]).then_inc(den_step, 1)
            v.wait_ge(den_step, b * 2 + 2)

        def dve_w1(v, b3, b1):
            if b3 is None:
                v.memset(acc[0], 0.0).then_inc(acc0_zero, 1)
            if b1 is None:
                for c in range(NG):
                    dve_last_ln2(v, b3, c)
                return
            for s in range(NS):
                if b3 is not None:
                    if s == STRIP_NO[(NG - 1, NG - 2, 0)]:
                        v.wait_ge(var_ready[1], b3 + 1)
                    if s == STRIP_NO[(NG - 1, NG - 1, 0)]:
                        v.wait_ge(out_stored, b3 * 16 + 16)
                if s in DEGREES_AT:
                    dve_degrees(v, b1, DEGREES_AT[s], 0)
                dve_s_strip(v, b1, s)
                if s in DEGREES_AT:
                    dve_degrees(v, b1, DEGREES_AT[s], 1)
                if s > 0:
                    dve_k_strip(v, b1, s - 1)
                if s in DEGREES_AT:
                    dve_degrees(v, b1, DEGREES_AT[s], 2)
                for i, j in UPPER_AFTER.get(s, ()):
                    dve_upper_sums(v, b1, i, j)
                if b3 is not None:
                    if s == LN2_START_AT:
                        dve_ln2_start(v, b3)
                    if s == LN2_START_AT + 1:
                        dve_ln2_scale(v, b3)
                    if s == LN2_START_AT + 2:
                        dve_ln2_no_nan(v, b3)
                    if s == LN2_MEAN_AFTER:
                        dve_ln2_mean(v, b3)
                    if s == LN2_VAR_AFTER:
                        dve_ln2_var(v, b3)
                if s == LAST_UPPER_AFTER:
                    dve_upper_sums(v, b1, 0, NG - 1)
                if s in KEEP_AFTER:
                    dve_keep_sums(v, b1, KEEP_AFTER[s])
            dve_k_strip(v, b1, NS - 1)
            dve_degrees(v, b1, NG - 1, 0)
            dve_keep_sums(v, b1, NG - 1)
            dve_degrees(v, b1, NG - 1, 1)
            dve_degrees(v, b1, NG - 1, 2)

        def pool_setup(g):
            g.memset(ident[:, :], 1.0).then_inc(ident_made, 1)
            g.wait_ge(ident_made, 1)
            g.affine_select(ident[:, :], ident[:, :], pattern=[[1, P]], compare_op=ALU.is_equal, fill=0.0,
                            base=0, channel_multiplier=-1).then_inc(ident_made, 1)

        def pool_z(g, b):
            g.wait_ge(z_in, b * 16 + 16)
            for n in range(NG):
                g.wait_ge(deg_step, (b * NG + n) * 3 + 3)
                g.tensor_tensor(of_group(d_sb, n), of_group(deg, n), minus_half[:, 0:G], ALU.pow).then_inc(d_ready, 1)
                g.wait_ge(d_ready, b * NG + n + 1)
                g.tensor_tensor(chunk(z_sb, n), chunk(z_sb, n), spread(of_group(d_sb, n), G), ALU.mult).then_inc(z_ready, 1)

        def pool_rstd1(g, b):
            for c in range(NG):
                g.wait_ge(var_ready[0], b * NG + c + 1)
                if c >= 2:
                    g.wait_ge(ln_ready[0], b * NG + c - 1)
                g.tensor_tensor(rstd[:, c % 2, :], var[:, c % 2, :], minus_half[:, 0:G],
                                ALU.pow).then_inc(rstd_ready[0], 1)

        def pool_ln2(g, b):
            g.wait_ge(ln_step[1], b * LN2_STEPS + 5)
            g.tensor_tensor(res2, res2, z_sb[:, :, :], ALU.add).then_inc(ln_pool, 1)
            g.wait_ge(ln_step[1], b * LN2_STEPS + 7)
            g.tensor_tensor(res2, res2, spread(mean2[:, :], NB), ALU.subtract).then_inc(ln_pool, 1)
            g.wait_ge(ln_pool, b * 3 + 2)
            g.tensor_tensor(sq2, res2, res2, ALU.mult).then_inc(ln_pool, 1)
            g.wait_ge(var_ready[1], b + 1)
            g.tensor_tensor(rstd2[:, :], var2[:, :], minus_half[:, :], ALU.pow).then_inc(rstd_ready[1], 1)
            g.wait_ge(rstd_ready[1], b + 1)
            g.tensor_tensor(res2, res2, spread(rstd2[:, :], NB), ALU.mult).then_inc(ln_ready[1], 1)

        def sp_w(sp, b, j, b3=None):
            if b3 is not None:
                sp.wait_ge(rows_freed, b3 * NG + j + 1)
            for n in range(j * G, (j + 1) * G):
                sp.dma_start(w_sb[:, n, 0:(j + 1) * SW], adj_v[b, :, n, 0:(j + 1) * SW]).then_inc(w_row[n], 16)
            if b3 is not None and j > 0:
                sp.wait_ge(freed, b3 * (NG - 1) + j)
            for i in range(j):
                sp.dma_start(w_sb[:, i * G:(i + 1) * G, j * SW:(j + 1) * SW],
                             adj_v[b, :, i * G:(i + 1) * G, j * SW:(j + 1) * SW]).then_inc(w_col[(i, j)], 16)

        def sp_move(sp, b, j):
            sp.dma_start(u_move[j % 2], u_scratch[:, j * SW:(j + 1) * SW]).then_inc(move_in[j % 2], 16)

        def sp_w1(sp, b3, b1):
            if b3 is None:
                for j in range(2):
                    sp_w(sp, b1, j)
                sp.wait_ge(u_kept, NG)
                sp.dma_start(u_scratch[:, :], move_all).then_inc(u_stored, 16)
                sp.wait_ge(u_stored, 16)
                for j in range(2):
                    sp_move(sp, b1, j)
                sp_w(sp, b1, 2)
                sp.wait_ge(u_kept, 2 * NG)
                sp.wait_ge(v_ready, STRIP_NO[(1, 0, 0)])
                sp_move(sp, b1, 2)
                sp_w(sp, b1, 3)
                sp.wait_ge(v_ready, STRIP_NO[(2, 0, 0)])
                sp_move(sp, b1, 3)
                sp.dma_start(z_sb[:, :, :], x_v[b1, :, :, :]).then_inc(z_in, 16)
                return
            if b1 is None:
                for c in range(NG):
                    sp.wait_ge(ln_ready[1], b3 + c + 1)
                    sp.dma_start(out_v[b3, :, c * G:(c + 1) * G, :], chunk(res2, c)).then_inc(out_stored, 16)
                return
            if b1 is not None:
                for j in range(NG):
                    sp_w(sp, b1, j, b3)
                    if j >= 2:
                        sp.wait_ge(v_ready, b1 * NS + STRIP_NO[(j - 1, 0, 0)])
                        sp_move(sp, b1, j)
            sp.wait_ge(ln_pool, b3 * 3 + 1)
            sp.dma_start(z_sb[:, :, :], x_v[b1, :, :, :]).then_inc(z_in, 16)
            sp.wait_ge(ln_ready[1], b3 + 1)
            sp.dma_start(out_v[b3, :, :, :], res2).then_inc(out_stored, 16)

        def sp_p2(sp, b):
            sp.wait_ge(col_turned, (b + 1) * len(COL_PARTS))
            for j in range(2):
                sp_move(sp, b, j)
            sp.wait_ge(scratch_free, b + 1)
            sp.dma_start(x_res, x_v[b, :, :, :]).then_inc(xres_in, 16)

        block = ctx.enter_context(nc.Block())

        @block.tensor
        def _(pe):
            pe_setup(pe)
            pe.wait_ge(const_made, 9)
            pe.wait_ge(ident_made, 2)
            begun = set()
            pe_w1(pe, None, 0, begun)
            pe_p2(pe, 0, begun)
            with pe.Fori(0, B - 1, 1) as b:
                begun = set()
                pe_w1(pe, b, b + 1, begun)
                pe_p2(pe, b + 1, begun)
            pe_w1(pe, B - 1, None, set())

        @block.scalar
        def _(act):
            act_setup(act)
            act_w1(act, None, 0)
            act_p2(act, 0)
            with act.Fori(0, B - 1, 1) as b:
                act_w1(act, b, b + 1)
                act_p2(act, b + 1)
            act_w1(act, B - 1, None)

        @block.vector
        def _(v):
            dve_setup(v)
            dve_w1(v, None, 0)
            dve_p2(v, 0)
            with v.Fori(0, B - 1, 1) as b:
                dve_w1(v, b, b + 1)
                dve_p2(v, b + 1)
            dve_w1(v, B - 1, None)

        @block.gpsimd
        def _(g):
            pool_setup(g)
            pool_z(g, 0)
            pool_rstd1(g, 0)
            with g.Fori(0, B - 1, 1) as b:
                pool_ln2(g, b)
                pool_z(g, b + 1)
                pool_rstd1(g, b + 1)
            for c in range(NG):
                g.wait_ge(var_ready[1], B - 1 + c + 1)
                g.tensor_tensor(rstd2[:, c * G:(c + 1) * G], var2[:, c * G:(c + 1) * G], minus_half[:, 0:G],
                                ALU.pow).then_inc(rstd_ready[1], 1)

        @block.sync
        def _(sp):
            sp.dma_start(u_nat, u.rearrange("(n p) r -> p n r", p=P)).then_inc(small_in, 16)
            sp.dma_start(scale_sb[:, :], w_scale.to_broadcast([P, 1])).then_inc(small_in, 16)
            sp_w1(sp, None, 0)
            sp_p2(sp, 0)
            with sp.Fori(0, B - 1, 1) as b:
                sp_w1(sp, b, b + 1)
                sp_p2(sp, b + 1)
            sp_w1(sp, B - 1, None)
            sp.wait_ge(out_stored, 16 * (B - 1 + NG))
            for i in range(2):
                sp.wait_ge(move_in[i], 32 * B + 16)


def kernel(**inputs):
    import numpy as _np
    import concourse.bacc as _bacc
    from concourse import mybir as _mybir
    from concourse.bass_utils import run_bass_kernel_spmd as _run

    nc = _bacc.Bacc("TRN2", target_bir_lowering=False, num_devices=1)
    arrays, args = {}, []
    for name in ("x", "adj", "L0_gnn_U", "L0_gnn_w_scale"):
        a = _np.ascontiguousarray(inputs[name])
        if name == "L0_gnn_w_scale":
            a = a.reshape(1, 1)
        arrays[f"in_{name}"] = a
        args.append(nc.dram_tensor(f"in_{name}", a.shape, _mybir.dt.from_np(a.dtype), kind="ExternalInput").ap())
    args.append(nc.dram_tensor("out_x", (B, N, C), F32, kind="ExternalOutput").ap())
    args.append(nc.dram_tensor("u_scratch", (P, N), BF16, kind="Internal").ap())
    build(nc, *args)
    r = _run(nc, [arrays], core_ids=[0])
    return r.results[0]["out_x"]
```
